# Optimizing a Trainium2 kernel written in Bass

```python
import numpy as np
import jax
import jax.numpy as jnp

def _softmax(x, axis=-1):
    return jax.nn.softmax(x, axis=axis)

def _gelu(x):
    return jax.nn.gelu(x, approximate=True)

def _silu(x):
    return jax.nn.silu(x)

def _sigmoid(x):
    return jax.nn.sigmoid(x)

def _layernorm(x, axis=-1, eps=1e-05):
    m = jnp.mean(x, axis=axis, keepdims=True)
    v = jnp.var(x, axis=axis, keepdims=True)
    return (x - m) / jnp.sqrt(v + eps)

def _scatter_add(tgt, idx, src, axis=0):
    return tgt.at[idx].add(src)

def _segment_sum(src, seg, n):
    return jax.ops.segment_sum(src, seg, n)
kernel_name = 'mk_seq_postln_d1_jaxref_r8_1ee367'

def setup_inputs(seed: int=0):
    np.random.seed(seed)
    _w = jnp.asarray

    def _L0_attn_setup():
        import jax, jax.numpy as jnp
        import numpy as np
        K_FACTOR = 0.5
        key = jax.random.key(seed)
        k1, k2, k3, k4 = jax.random.split(key, 4)
        B, S, H, I = (1, 256, 512, 1376)
        x = jax.random.normal(k1, (B, S, H), dtype=jnp.float32)
        w_gate = jax.random.normal(k2, (I, H), dtype=jnp.float32) * 0.02
        w_up = jax.random.normal(k3, (I, H), dtype=jnp.float32) * 0.02
        w_down = jax.random.normal(k4, (H, I), dtype=jnp.float32) * 0.02
        return {'x': x, 'w_gate': w_gate, 'w_up': w_up, 'w_down': w_down}
    _L0_attn_in = _L0_attn_setup()

    def _L0_ffn_setup():
        import jax, jax.numpy as jnp
        import numpy as np
        HD, M = (512, 1792)
        key = jax.random.key(seed)
        k_x, k_g, k_u, k_d = jax.random.split(key, 4)
        scale = 1.0 / np.sqrt(HD)
        x = jax.random.normal(k_x, (4, 256, HD), dtype=jnp.float16)
        W_gate = jax.random.normal(k_g, (M, HD), dtype=jnp.float16) * jnp.float16(scale)
        W_up = jax.random.normal(k_u, (M, HD), dtype=jnp.float16) * jnp.float16(scale)
        W_down = jax.random.normal(k_d, (HD, M), dtype=jnp.float16) * jnp.float16(1.0 / np.sqrt(M))
        return {'x': x, 'W_gate': W_gate, 'W_up': W_up, 'W_down': W_down}
    _L0_ffn_in = _L0_ffn_setup()
    _d = {'L0_attn_x': _L0_attn_in['x'], 'L0_attn_w_gate': _L0_attn_in['w_gate'], 'L0_attn_w_up': _L0_attn_in['w_up'], 'L0_attn_w_down': _L0_attn_in['w_down'], 'L0_ffn_W_gate': _L0_ffn_in['W_gate'], 'L0_ffn_W_up': _L0_ffn_in['W_up'], 'L0_ffn_W_down': _L0_ffn_in['W_down']}
    _x0 = _d['L0_attn_x']
    _d['L0_attn_x'] = jax.random.normal(jax.random.fold_in(jax.random.key(seed), 1), (4, 256, 512), dtype=_x0.dtype)
    del _x0
    return _d

def reference(L0_attn_x, L0_attn_w_gate, L0_attn_w_up, L0_attn_w_down, L0_ffn_W_gate, L0_ffn_W_up, L0_ffn_W_down):

    def _L0_attn_ref(x, w_gate, w_up, w_down):
        import jax, jax.numpy as jnp
        import numpy as np
        K_FACTOR = 0.5
        s = jax.nn.silu(jnp.einsum('bsh,ih->bsi', x, w_gate))
        B, S, I = s.shape
        k = int(K_FACTOR * I)
        _, idx = jax.lax.top_k(-jnp.abs(s), k)
        flat = s.reshape(B * S, I)
        rows = jnp.arange(B * S)[:, None]
        flat = flat.at[rows, idx.reshape(B * S, k)].set(0.0)
        s = flat.reshape(B, S, I)
        s = s * jnp.einsum('bsh,ih->bsi', x, w_up)
        return jnp.einsum('bsi,hi->bsh', s, w_down)

    def _L0_ffn_ref(x, W_gate, W_up, W_down):
        import jax, jax.numpy as jnp
        import numpy as np
        HD, M = (512, 1792)
        gate = jnp.einsum('bsh,mh->bsm', x, W_gate)
        up = jnp.einsum('bsh,mh->bsm', x, W_up)
        h = jax.nn.silu(gate) * up
        out = jnp.einsum('bsm,hm->bsh', h, W_down)
        return out
    x = L0_attn_x
    x = _layernorm(x + _L0_attn_ref(x, L0_attn_w_gate, L0_attn_w_up, L0_attn_w_down), axis=-1)
    x = _layernorm(x + _L0_ffn_ref(x, L0_ffn_W_gate, L0_ffn_W_up, L0_ffn_W_down), axis=-1)
    return x

_drawn_inputs = setup_inputs


def setup_inputs(seed=0):
    import zlib

    import numpy as np

    out = dict(_drawn_inputs(seed))
    spreads = {}
    factors = {}
    for name, (base, spread) in spreads.items():
        noise = np.random.default_rng([zlib.crc32(name.encode()), seed]).standard_normal(out[name].shape)
        drawn = base * np.exp(spread * noise) if base else spread * noise
        out[name] = jnp.asarray(drawn.astype(out[name].dtype))
    for name, factor in factors.items():
        out[name] = (out[name] * factor).astype(out[name].dtype)
    return out
```

```python
import concourse.bass as bass
from concourse import mybir
from contextlib import ExitStack


def build(nc, x, w_gate, w_up, w_down, v_gate, v_up, v_down, out):
    f32, f32r = mybir.dt.float32, mybir.dt.float32r
    f16, i32, i8 = mybir.dt.float16, mybir.dt.int32, mybir.dt.int8
    ALU, ACT = mybir.AluOpType, mybir.ActivationFunctionType

    P = 128
    HD = x.shape[2]
    TOK = x.shape[0] * x.shape[1]
    NT = TOK // P
    KB = HD // P
    I = w_gate.shape[0]
    IB = -(-I // P)
    IW = [min(P, I - P * b) for b in range(IB)]
    CH = [(c, min(c + 512, I)) for c in range(0, I, 512)]
    NC_ = len(CH)
    GRP = [list(range(4 * g, min(4 * g + 4, IB))) for g in range(NC_)]
    ZERO = I // 2
    M2 = v_gate.shape[0]
    MB = M2 // P
    HALF = TOK // 2
    TH = HALF // P
    UP = 1024.0
    EPS = 1e-5
    START, SLOPE, AIM, NEAR = 0.782, 655.0, ZERO + 8, 7.5
    PASSES = 4

    xf = x.rearrange("b s h -> (b s) h")
    of = out.rearrange("b s h -> (b s) h")
    x2_dram = nc.dram_tensor("x2_scratch", [TOK, HD], f32).ap()

    ctx = ExitStack()
    with ctx:
        base = -(-nc.sbuf_base // 64) * 64
        at = [base]

        def place(name, shape, dt, size, offset=None):
            if offset is None:
                offset = at[0]
                at[0] += -(-size // 32) * 32
            return nc.alloc_sbuf_tensor_at(name, [P] + shape, dt, offset=offset), offset

        wg_hi, A0 = place("wg_hi", [KB, I], f32r, KB * I * 4)
        wg_lo, _ = place("wg_lo", [KB, I], f32r, KB * I * 4)
        wu_hi, B0 = place("wu_hi", [KB, I], f32r, KB * I * 4)
        wu_lo, _ = place("wu_lo", [KB, I], f32r, KB * I * 4)
        wd_hi, C0 = place("wd_hi", [IB, HD], f32r, IB * HD * 4)
        wd_lo, _ = place("wd_lo", [IB, HD], f32r, IB * HD * 4)
        x16, X0 = place("x16", [NT * 2 * HD], f16, NT * 2 * HD * 2)
        nat = [place("nat0", [2048], f32, 0, X0)[0], place("nat1", [2048], f32, 0, X0 + 8192)[0]]
        x_in = [place(f"x_in{i}", [HD], f32, HD * 4)[0] for i in range(2)]
        x_res, _ = place("x_res", [HD], f32, HD * 4)
        x2, _ = place("x2", [HD], f32, HD * 4)
        xt_hi = [place(f"xt_hi{i}", [KB, P], f32r, HD * 4)[0] for i in range(2)]
        xt_lo = [place(f"xt_lo{i}", [KB, P], f32r, HD * 4)[0] for i in range(2)]
        s0, S0 = place("s0", [I], f32, I * 4)
        s1, _ = place("s1", [I], f32, I * 4)
        a0, _ = place("a0", [I], f32, I * 4)
        a1, _ = place("a1", [I], f32, I * 4)
        s_buf, a_buf = [s0, s1], [a0, a1]
        h_buf, _ = place("h_buf", [I], f32, I * 4)
        ht_hi = [place(f"ht_hi{i}", [4, P], f32r, 2048)[0] for i in range(2)]
        ht_lo = [place(f"ht_lo{i}", [4, P], f32r, 2048)[0] for i in range(2)]
        signs, _ = place("signs", [I], i8, I)
        ident, _ = place("ident", [P], f32, P * 4)
        ident16, _ = place("ident16", [P], f16, P * 2)
        rank, _ = place("rank", [17], f32, 17 * 4)
        top, _ = place("top", [16], f32, 64)
        small, _ = place("small", [64], f32, 256)
        ints, _ = place("ints", [8], i32, 32)
        nat.append(place("nat2", [2048], f32, 8192)[0])
        assert at[0] <= nc.sbuf_usable_end, (at[0], nc.sbuf_usable_end)
        ng, _ = place("ng", [MB, HD], f16, 0, A0)
        nu, _ = place("nu", [MB, HD], f16, 0, A0 + MB * HD * 2)
        nd, _ = place("nd", [KB, M2], f16, 0, A0 + 2 * MB * HD * 2)
        vgu, _ = place("vgu", [2 * KB, M2], f16, 0, B0)
        res = [place(f"res{j}", [HD], f32, 0, B0 + 2 * KB * M2 * 2 + j * HD * 4)[0] for j in range(TH)]
        vd, _ = place("vd", [MB, HD], f32r, 0, C0)
        C1 = C0 + MB * HD * 4
        h2_hi = [place(f"h2_hi{i}", [HALF], f32r, 0, C1 + i * 2048)[0] for i in range(2)]
        h2_lo = [place(f"h2_lo{i}", [HALF], f32r, 0, C1 + 4096 + i * 2048)[0] for i in range(2)]
        sg = [place(f"sg{i}", [HALF], f32, 0, C1 + 8192 + i * 2048)[0] for i in range(2)]
        h2 = [place(f"h2{i}", [HALF], f32, 0, C1 + 12288 + i * 2048)[0] for i in range(2)]
        x2t, _ = place("x2t", [2, KB, TOK], f16, 0, S0)

        cols = iter(range(64))

        def col(n=1):
            c = [next(cols) for _ in range(n)]
            return small[:, c[0]:c[-1] + 1]

        half_c, one_c, good, keep, below, cnt, jj, jok = (col() for _ in range(8))
        abs_sum, sign_sum, err, far, step, neg_t, unit, unit2 = (col() for _ in range(8))
        start_c, unit_c, unit2_c, aim_c, minus_c = (col() for _ in range(5))
        pos_t = [col(), col()]
        stats, mv, rstd, var_e = col(6), col(2), col(), col()
        stats2, mv2, rstd2, var_e2 = col(6), [col(2) for _ in range(TH)], col(TH), col(TH)
        tie_m, le = col(), col()
        bit, found, tried, gain, n_good = (ints[:, i:i + 1] for i in range(5))

        def bank(name):
            return ctx.enter_context(nc.psum_tensor(name, [P, 512], f32))

        gu = [bank(f"gu{i}") for i in range(3)]
        tp = [bank(f"tp{i}") for i in range(3)]
        dn = bank("dn")
        xb = bank("xb")
        g2, u2, t2gu, t2d = gu[0], gu[1], gu[2], xb
        acc = [tp[0], tp[1], tp[2], dn]

        sem = {}

        def S(name):
            if name not in sem:
                sem[name] = ctx.enter_context(nc.semaphore(name))
            return sem[name]

        CR = {"u_mul": 3, "h_done": 3, "sel_done": 1, "y_done": 1, "ht_lo": 3, "d_mm": 2, "x2_saved": 16}

        def done(name, n):
            return n + CR.get(name, 0)

        STEPS = NT - 2

        def steps(eng, step_fn):
            with eng.Fori(0, STEPS - 1, 2) as i:
                step_fn(i, 0)
                step_fn(i + 1, 1)
            step_fn(STEPS, 0)
            step_fn(STEPS + 1, 1)

        def steps2(eng, fn, between=lambda: None, after=lambda half: None):
            for q in range(2):
                fn(q, q % 2, True)
            with eng.Fori(2, MB - 3, 2) as i:
                fn(i, 0, True)
                fn(i + 1, 1, True)
            fn(MB - 2, 0, False)
            between()
            fn(MB - 1, 1, False)
            after(0)
            for q in range(2):
                fn(MB + q, q, False)
            with eng.Fori(MB + 2, 2 * MB - 3, 2) as i:
                fn(i, 0, False)
                fn(i + 1, 1, False)
            fn(2 * MB - 2, 0, False)
            fn(2 * MB - 1, 1, False)
            after(1)

        def is_last(t, k):
            return isinstance(t, int) and t >= NT - k

        def nat_rows(src, b):
            return src[P * b:P * b + IW[b], :]

        NSLAB = 10

        def slab_view(n):
            return nat[n % 3]

        def prologue_groups():
            for w in range(2):
                for b in range(IB):
                    yield ("gu", w, b)
            for hb in range(KB):
                for g in range(NC_):
                    yield ("d", hb, g)

        GROUPS = list(prologue_groups())
        N_WG, N_WU, N_ALL = IB, 2 * IB, len(GROUPS)

        def slab_of(g):
            return 3 * g[1] + g[2] // 4 if g[0] == "gu" else 6 + g[1]

        last_group_of_slab = {slab_of(g): n for n, g in enumerate(GROUPS)}

        def group_dst(g):
            n = GROUPS.index(g)
            if g[0] == "gu":
                hi, lo = ((wg_hi, wg_lo), (wu_hi, wu_lo))[g[1]]
                b = g[2]
                c = slice(P * b, P * b + IW[b])
                src = tp[n % 3][:, :].rearrange("p (k c) -> p k c", k=KB)[:, :, 0:IW[b]]
                return hi[:, :, c], lo[:, :, c], src
            bl = GRP[g[2]]
            c = slice(P * g[1], P * g[1] + P)
            src = tp[n % 3][:, 0:P * len(bl)].rearrange("p (k c) -> p k c", c=P)
            return wd_hi[:, bl[0]:bl[-1] + 1, c], wd_lo[:, bl[0]:bl[-1] + 1, c], src

        vg_v = v_gate.rearrange("(m p) h -> p m h", p=P)
        vu_v = v_up.rearrange("(m p) h -> p m h", p=P)
        vd_v = v_down.rearrange("(b p) m -> p b m", p=P)
        NG_SPLIT = [0, 2, 7, MB]
        block = ctx.enter_context(nc.Block())

        @block.sync
        def _(eng):
            eng.nop().then_inc(S("x2_saved"), 16)
            for t in range(2):
                if t:
                    eng.wait_ge(S("x_loaded"), 16 * t)
                eng.dma_start(x_in[t][:, :], xf[P * t:P * t + P, :]).then_inc(S("x_loaded"), 16)
            for n in range(NSLAB):
                if n >= 3:
                    eng.wait_ge(S("w_tr"), last_group_of_slab[n - 3] + 1)
                dst, s = slab_view(n), S(f"slab{n}")
                if n < 6:
                    src = (w_gate, w_up)[n // 3]
                    bl = GRP[n % 3]
                    full = [b for b in bl if IW[b] == P]
                    eng.dma_start(dst[:, 0:HD * len(full)].rearrange("p (b h) -> p b h", h=HD),
                                  src[P * full[0]:P * full[-1] + P, :].rearrange("(b p) h -> p b h", p=P)
                                  ).then_inc(s, 16)
                    for b in bl[len(full):]:
                        o = HD * (b - bl[0])
                        eng.dma_start(dst[0:IW[b], o:o + HD], nat_rows(src, b)).then_inc(s, 16)
                else:
                    hb = n - 6
                    eng.dma_start(dst[:, 0:I], w_down[P * hb:P * hb + P, :]).then_inc(s, 16)

            def body(t, more):
                if more:
                    eng.wait_ge(S("x_tr"), t + 1)
                    eng.wait_ge(S("x_loaded"), 16 * t + 32)
                    dst = x_in_all(t)
                    eng.dma_start(dst, xf[bass.ds(t * P + 2 * P, P), :]).then_inc(S("x_loaded"), 16)
                eng.wait_ge(S("y_done"), t + 1)
                eng.dma_start(x_res[:, :], xf[bass.ds(t * P, P), :]).then_inc(S("xr_loaded"), 16)
                eng.wait_ge(S("x2_done"), t + 1)
                eng.dma_start(x2_dram[bass.ds(t * P, P), :], x2[:, :]).then_inc(S("x2_saved"), 16)

            def x_in_all(t):
                return x_in[par[0]][:, :]

            par = [0]
            with eng.Fori(0, STEPS - 1, 2) as i:
                for k in range(2):
                    par[0] = k
                    body(i + k, True)
            body(NT - 2, False)
            eng.wait_ge(S("g_mm"), 3 * NT)
            for n, (lo, hi) in enumerate(zip(NG_SPLIT, NG_SPLIT[1:])):
                eng.dma_start(ng[:, lo:hi, :], vg_v[:, lo:hi, :]).then_inc(S(f"n2_{n}"), 16)
                eng.dma_start(nu[:, lo:hi, :], vu_v[:, lo:hi, :]).then_inc(S(f"n2_{n}"), 16)
                if n == 0:
                    eng.dma_start(nd[:, :, :], vd_v).then_inc(S("nd"), 16)
            body(NT - 1, False)
            eng.wait_ge(S("x2_saved"), 16 * (NT + 1))
            eng.wait_ge(S("u_mm"), 3 * NT)
            for j in range(TH):
                eng.dma_start(res[j][:, :], x2_dram[P * j:P * j + P, :]).then_inc(S("res"), 16)
            for half in range(2):
                for j in range(TH):
                    t = TH * half + j
                    eng.wait_ge(S("o_done"), t + 1)
                    eng.dma_start(of[P * t:P * t + P, :], res[j][:, :]).then_inc(S("out"), 16)
                if half == 0:
                    eng.wait_ge(S("out"), 16 * TH)
                    for j in range(TH):
                        t = TH + j
                        eng.dma_start(res[j][:, :], x2_dram[P * t:P * t + P, :]).then_inc(S("res"), 16)
            eng.wait_ge(S("out"), 16 * NT)

        @block.gpsimd
        def _(eng):
            eng.memset(ident[:, :], 0.0)
            eng.memset(ident16[:, :], 0.0)
            eng.memset(half_c, -0.5)
            eng.memset(one_c, 1.0)
            eng.memset(minus_c, -1.0)
            eng.memset(start_c, -START / I)
            eng.memset(unit_c, -0.5 * START / I / SLOPE)
            eng.memset(unit2_c, -0.5 * 0.85 * START / I / SLOPE)
            eng.memset(aim_c, float(I - 2 * AIM))
            for k in range(17):
                eng.memset(rank[:, k:k + 1], float(k - 1))
            eng.drain()
            for m in (ident, ident16):
                eng.affine_select(out=m[:, :], in_=m[:, :], compare_op=ALU.not_equal, fill=1.0,
                                  base=0, pattern=[[-1, P]], channel_multiplier=1)
            eng.drain()
            eng.nop().then_inc(S("consts"), 1)

            def search(t, p):
                eng.wait_ge(S("abs_done"), t + 1)
                eng.tensor_tensor(unit, abs_sum, unit_c, ALU.mult)
                eng.tensor_tensor(unit2, abs_sum, unit2_c, ALU.mult)
                eng.tensor_tensor(neg_t, abs_sum, start_c, ALU.mult).then_inc(S("thr"), 1)
                eng.drain()
                for n in range(PASSES):
                    eng.wait_ge(S("counted"), t * PASSES + n + 1)
                    eng.tensor_tensor(err, sign_sum, aim_c, ALU.subtract)
                    eng.drain()
                    eng.tensor_scalar(far, err, err, 4 * NEAR * NEAR, ALU.mult, ALU.is_gt)
                    eng.tensor_scalar(step, err, unit if n < 2 else unit2, None, ALU.mult)
                    eng.drain()
                    last = n == PASSES - 1
                    ins = eng.tensor_scalar(neg_t, step, far, neg_t, ALU.mult, ALU.add)
                    if last:
                        eng.drain()
                        if p is not None:
                            eng.wait_ge(S("sel_done"), t)
                        ins = eng.tensor_tensor(pos_t[parity[0]], neg_t, minus_c, ALU.mult)
                    ins.then_inc(S("thr"), 1)
                    eng.drain()

            parity = [0]
            search(0, None)

            def step_fn(t, p):
                if not is_last(t, 1):
                    parity[0] = 1 - p
                    search(t + 1, p)
                eng.wait_ge(S("var_done"), t + 1)
                eng.tensor_tensor(rstd, var_e, half_c, ALU.pow).then_inc(S("rstd"), 1)

            steps(eng, step_fn)
            for t in range(NT):
                eng.wait_ge(S("var2_done"), t + 1)
                j = t % TH
                eng.tensor_tensor(rstd2[:, j:j + 1], var_e2[:, j:j + 1], half_c, ALU.pow).then_inc(S("rstd2"), 1)

        @block.scalar
        def _(eng):
            def x_hi(t, p):
                eng.wait_ge(S("x_tr"), t + 1)
                eng.activation(xt_hi[p][:, :, :], xb[:, :].rearrange("p (k c) -> p k c", k=KB),
                               ACT.Copy).then_inc(S("xt_hi"), 1)

            def weights_hi(n):
                hi, _, src = group_dst(GROUPS[n])
                eng.wait_ge(S("w_tr"), n + 1)
                eng.activation(hi, src, ACT.Copy).then_inc(S("w_hi"), 1)

            def silu(t, p, c):
                lo, hi = CH[c]
                eng.wait_ge(S("g_mm"), 3 * t + c + 1)
                eng.activation(s_buf[p][:, lo:hi], gu[c][:, 0:hi - lo], ACT.Silu).then_inc(S("g_act"), 1)

            def absolute(t, p):
                eng.wait_ge(S("g_act"), 3 * t + 3)
                eng.activation(a_buf[p][:, :], s_buf[p][:, :], ACT.Abs,
                               accum_out=abs_sum).then_inc(S("abs_done"), 1)

            def count(t, p, n):
                eng.wait_ge(S("thr"), t * (PASSES + 1) + n + 1)
                eng.wait_ge(S("abs_done"), t + 1)
                eng.activation(signs[:, :], a_buf[p][:, :], ACT.Sign, bias=neg_t,
                               accum_out=sign_sum).then_inc(S("counted"), 1)

            def h_hi(t, g, b):
                eng.wait_ge(S("ht_tr"), 3 * t + g + 1)
                eng.wait_ge(S("d_mm"), 3 * t + g + 1)
                w = P * len(GRP[g])
                eng.activation(ht_hi[b][:, 0:len(GRP[g]), :],
                               tp[g][:, 0:w].rearrange("p (k c) -> p k c", c=P),
                               ACT.Copy).then_inc(S("ht_hi"), 1)

            x_hi(0, 0)
            x_hi(1, 1)
            for n in range(N_WG):
                weights_hi(n)
            for c in range(NC_):
                silu(0, 0, c)
            absolute(0, 0)
            for n in range(N_WG, N_ALL):
                k = n - N_WG
                if k % 3 == 0 and k // 3 < PASSES:
                    count(0, 0, k // 3)
                weights_hi(n)

            def step_fn(t, p):
                q = 1 - p
                if not is_last(t, 1):
                    eng.wait_ge(S("h_done"), 3 * t + 3)
                    for c in range(NC_):
                        silu(t + 1, q, c)
                    absolute(t + 1, q)
                    count(t + 1, q, 0)
                    count(t + 1, q, 1)
                if not is_last(t, 2):
                    eng.wait_ge(S("u_mm"), 3 * t + 3)
                    x_hi(t + 2, p)
                h_hi(t, 0, p)
                h_hi(t, 1, q)
                if not is_last(t, 1):
                    count(t + 1, q, 2)
                h_hi(t, 2, p)
                if not is_last(t, 1):
                    count(t + 1, q, 3)

            steps(eng, step_fn)

            def x2t_copy(t):
                eng.wait_ge(S("x2t_tr"), t + 1)
                src = t2gu[:, :].bitcast(f16).rearrange("p (j c) -> p j c", c=P)
                eng.activation(x2t[:, :, :, P * t:P * t + P].rearrange("p a k c -> p (a k) c"), src,
                               ACT.Copy).then_inc(S("x2t_ev"), 1)

            def vgu_copy(m):
                eng.wait_ge(S("vgu_tr"), m + 1)
                src = t2gu[:, :].bitcast(f16).rearrange("p (j c) -> p j c", c=P)
                eng.activation(vgu[:, :, bass.ds(m * P, P)], src, ACT.Copy).then_inc(S("vgu_ev"), 1)

            def gate2(q, p):
                eng.wait_ge(S("g2_mm"), q + 1)
                if not (isinstance(q, int) and q < 2):
                    eng.wait_ge(S("h2_done"), q - 1)
                eng.activation(sg[p][:, :], g2[:, :], ACT.Silu, scale=1.0 / UP).then_inc(S("sg_done"), 1)

            def h2_high(q, p):
                eng.wait_ge(S("h2_done"), q + 1)
                if not (isinstance(q, int) and q < 2):
                    eng.wait_ge(S("dn_mm"), 4 * q - 4)
                eng.activation(h2_hi[p][:, :], h2[p][:, :], ACT.Copy).then_inc(S("h2_hi"), 1)

            eng.wait_ge(S("h_done"), done("h_done", 3 * NT))
            for t in range(TH):
                x2t_copy(t)
            vgu_copy(0)
            vgu_copy(1)
            eng.wait_ge(S("d_mm"), done("d_mm", 3 * NT))

            def step2(q, p, more):
                gate2(q, p)
                if more:
                    vgu_copy(q + 2)
                h2_high(q, p)

            steps2(eng, step2, lambda: [x2t_copy(t) for t in range(TH, NT)])

        @block.vector
        def _(eng):
            v = nc.vector
            for name, n in CR.items():
                if name in ("u_mul", "h_done", "sel_done", "y_done", "ht_lo"):
                    eng.nop().then_inc(S(name), n)

            def x_low(t, p):
                eng.wait_ge(S("xt_hi"), t + 1)
                v.tensor_tensor(xt_lo[p][:, :, :], xb[:, :].rearrange("p (k c) -> p k c", k=KB),
                                xt_hi[p][:, :, :], ALU.subtract).then_inc(S("xt_lo"), 1)

            def weights_lo(n):
                hi, lo, src = group_dst(GROUPS[n])
                eng.wait_ge(S("w_hi"), n + 1)
                v.tensor_tensor(lo, src, hi, ALU.subtract).then_inc(S("w_lo"), 1)

            def select(t, p):
                a = a_buf[p]
                eng.wait_ge(S("thr"), t * (PASSES + 1) + PASSES + 1)
                eng.wait_ge(S("abs_done"), t + 1)
                v.tensor_scalar(h_buf[:, :], a[:, :], pos_t[p], None, ALU.is_lt, ALU.add, accum_out=cnt)
                eng.drain()
                v.scalar_tensor_tensor(h_buf[:, :], a[:, :], pos_t[p], a[:, :], ALU.is_lt, ALU.mult)
                eng.drain()
                v.tensor_scalar(jj, cnt, float(ZERO + 1), None, ALU.subtract)
                v.max(top[:, 0:8], h_buf[:, :])
                eng.drain()
                v.tensor_scalar(jok, jj, 14.5, None, ALU.is_le)
                v.match_replace(h_buf[:, :], top[:, 0:8], h_buf[:, :], -1.0)
                eng.drain()
                v.max(top[:, 8:16], h_buf[:, :])
                eng.drain()
                v.scalar_tensor_tensor(h_buf[:, 0:16], rank[:, 1:17], jj, top[:, :], ALU.is_equal,
                                       ALU.mult, accum_out=keep)
                v.scalar_tensor_tensor(h_buf[:, 16:32], rank[:, 0:16], jj, top[:, :], ALU.is_equal,
                                       ALU.mult, accum_out=below)
                eng.drain()
                v.tensor_scalar(good, keep, below, jok, ALU.is_gt, ALU.mult).then_inc(S("sel_done"), 1)

            def up_times_s(t, p, c):
                lo, hi = CH[c]
                eng.wait_ge(S("u_mm"), 3 * t + c + 1)
                eng.wait_ge(S("abs_done"), t + 1)
                v.tensor_tensor(s_buf[p][:, lo:hi], gu[c][:, 0:hi - lo], s_buf[p][:, lo:hi],
                                ALU.mult).then_inc(S("u_mul"), 1)

            def settle(t, p):
                a, found_f = a_buf[p], found.bitcast(f32)
                eng.wait_ge(S("flag_mm"), t + 1)
                v.tensor_copy(n_good[0:1, :], xb[0:1, 0:1]).then_inc(S("flag_read"), 1)
                eng.drain()
                n = eng.value_load(n_good[0:1, :], min_val=0, max_val=P)
                with eng.If(n != P):
                    v.memset(bit.bitcast(f32), 2.0)
                    v.memset(found, 0)
                    eng.drain()
                    with eng.Fori(0, 31):
                        v.tensor_tensor(tried, found, bit, ALU.bitwise_or)
                        eng.drain()
                        v.tensor_scalar(h_buf[:, :], a[:, :], tried.bitcast(f32), None, ALU.is_lt,
                                        ALU.add, accum_out=cnt)
                        eng.drain()
                        v.tensor_scalar(le, cnt, ZERO - 0.5, None, ALU.is_le)
                        eng.drain()
                        v.tensor_scalar(gain, bit, le, None, ALU.mult)
                        eng.drain()
                        v.tensor_tensor(found, found, gain, ALU.bitwise_or)
                        v.tensor_scalar(bit, bit, 1, None, ALU.logical_shift_right)
                        eng.drain()
                    v.tensor_scalar(h_buf[:, :], a[:, :], found_f, None, ALU.is_lt, ALU.add, accum_out=cnt)
                    eng.drain()
                    v.tensor_scalar(tie_m, cnt, -1.0, float(ZERO), ALU.mult, ALU.add)
                    v.tensor_scalar(h_buf[:, :], a[:, :], found_f, None, ALU.is_equal)
                    eng.drain()
                    v.tensor_tensor_scan(h_buf[:, :], h_buf[:, :], h_buf[:, :], 0.0, ALU.add, ALU.max)
                    eng.drain()
                    v.tensor_scalar(h_buf[:, :], h_buf[:, :], tie_m, None, ALU.is_le)
                    eng.drain()
                    v.scalar_tensor_tensor(h_buf[:, :], a[:, :], found_f, h_buf[:, :], ALU.is_equal, ALU.mult)
                    eng.drain()
                    v.scalar_tensor_tensor(a[:, :], h_buf[:, :], -3e38, a[:, :], ALU.mult, ALU.add)
                    v.tensor_copy(keep, found_f)
                    eng.drain()
                with eng.Else():
                    eng.nop()

            def hidden(t, p, c):
                lo, hi = CH[c]
                v.scalar_tensor_tensor(h_buf[:, lo:hi], a_buf[p][:, lo:hi], keep, s_buf[p][:, lo:hi],
                                       ALU.is_ge, ALU.mult).then_inc(S("h_done"), 1)

            def h_low(t, g, b):
                eng.wait_ge(S("ht_hi"), 3 * t + g + 1)
                w, n = P * len(GRP[g]), len(GRP[g])
                v.tensor_tensor(ht_lo[b][:, 0:n, :], tp[g][:, 0:w].rearrange("p (k c) -> p k c", c=P),
                                ht_hi[b][:, 0:n, :], ALU.subtract).then_inc(S("ht_lo"), 1)

            def norm(t):
                eng.wait_ge(S("d_mm"), done("d_mm", 3 * t + 3))
                eng.wait_ge(S("xr_loaded"), 16 * t + 16)
                eng.wait_ge(S("x2_saved"), 16 * t + 16)
                v.tensor_tensor(x2[:, :], dn[:, :], x_res[:, :], ALU.add).then_inc(S("y_done"), 1)
                eng.drain()
                v.bn_stats(stats, x2[:, :])
                eng.drain()
                v.bn_aggr(mv, stats)
                eng.drain()
                v.tensor_scalar(var_e, mv[:, 1:2], EPS, None, ALU.add).then_inc(S("var_done"), 1)
                eng.wait_ge(S("rstd"), t + 1)
                v.tensor_scalar(x2[:, :], x2[:, :], mv[:, 0:1], rstd, ALU.subtract, ALU.mult
                                ).then_inc(S("x2_done"), 1)
                eng.drain()
                hi = x16[:, bass.ds(t * 2 * HD, HD)]
                lo = x16[:, bass.ds(t * 2 * HD + HD, HD)]
                v.tensor_scalar(hi, x2[:, :], UP, None, ALU.mult)
                eng.drain()
                v.scalar_tensor_tensor(lo, x2[:, :], UP, hi, ALU.mult, ALU.subtract).then_inc(S("x16"), 1)

            x_low(0, 0)
            x_low(1, 1)
            for n in range(N_WU):
                weights_lo(n)
            eng.wait_ge(S("consts"), 1)
            select(0, 0)
            for n in range(N_WU, N_ALL):
                weights_lo(n)

            def step_fn(t, p):
                q = 1 - p
                up_times_s(t, p, 0)
                up_times_s(t, p, 1)
                settle(t, p)
                eng.drain()
                hidden(t, p, 0)
                hidden(t, p, 1)
                up_times_s(t, p, 2)
                eng.drain()
                hidden(t, p, 2)
                if not is_last(t, 2):
                    x_low(t + 2, p)
                h_low(t, 0, p)
                h_low(t, 1, q)
                h_low(t, 2, p)
                if not is_last(t, 1):
                    select(t + 1, q)
                norm(t)

            steps(eng, step_fn)

            def vd_copy(m):
                eng.wait_ge(S("vd_tr"), m + 1)
                v.tensor_copy(vd[:, bass.ds(m, 1), :].rearrange("p a c -> p (a c)"),
                              t2d[:, 0:HD // 2].bitcast(f16)).then_inc(S("vd_ev"), 1)

            def h2_mul(q, p):
                eng.wait_ge(S("sg_done"), q + 1)
                eng.wait_ge(S("u2_mm"), q + 1)
                if not (isinstance(q, int) and q < 2):
                    eng.wait_ge(S("h2_hi"), q - 1)
                v.scalar_tensor_tensor(h2[p][:, :], u2[:, :], 1.0 / UP, sg[p][:, :], ALU.mult,
                                       ALU.mult).then_inc(S("h2_done"), 1)

            def h2_low(q, p):
                eng.wait_ge(S("h2_hi"), q + 1)
                v.tensor_tensor(h2_lo[p][:, :], h2[p][:, :], h2_hi[p][:, :],
                                ALU.subtract).then_inc(S("h2_lo"), 1)

            in_half = [0]

            def step2(q, p, more):
                if in_half[0] == 0:
                    vd_copy(q)
                h2_mul(q, p)
                h2_low(q, p)

            def finish(half):
                in_half[0] = 1
                for j in range(TH):
                    t = TH * half + j
                    eng.wait_ge(S("dn_mm"), 4 * MB * (half + 1) - TH + j + 1)
                    if j == 0:
                        eng.wait_ge(S("res"), 16 * TH * (half + 1))
                    v.tensor_tensor(res[j][:, :], acc[j][:, :], res[j][:, :], ALU.add).then_inc(S("y2_done"), 1)
                    eng.drain()
                    v.bn_stats(stats2, res[j][:, :])
                    eng.drain()
                    v.bn_aggr(mv2[j], stats2)
                    eng.drain()
                    v.tensor_scalar(var_e2[:, j:j + 1], mv2[j][:, 1:2], EPS, None, ALU.add
                                    ).then_inc(S("var2_done"), 1)
                for j in range(TH):
                    t = TH * half + j
                    eng.wait_ge(S("rstd2"), t + 1)
                    v.tensor_scalar(res[j][:, :], res[j][:, :], mv2[j][:, 0:1], rstd2[:, j:j + 1],
                                    ALU.subtract, ALU.mult).then_inc(S("o_done"), 1)

            steps2(eng, step2, after=finish)

        @block.tensor
        def _(eng):
            eng.nop().then_inc(S("d_mm"), CR["d_mm"])

            def x_transpose(t, p):
                eng.wait_ge(S("x_loaded"), 16 * t + 16)
                if isinstance(t, int) and t < 2:
                    if t:
                        eng.wait_ge(S("xt_lo"), t)
                else:
                    eng.wait_ge(S("flag_read"), t - 1)
                for k in range(KB):
                    ins = eng.transpose(xb[:, P * k:P * k + P], x_in[p][:, P * k:P * k + P], ident[:, :])
                ins.then_inc(S("x_tr"), 1)

            def weights_transpose(n):
                g = GROUPS[n]
                s = slab_of(g)
                src, bk = slab_view(s), tp[n % 3]
                eng.wait_ge(S(f"slab{s}"), 32 if s < 6 and s % 3 == 2 else 16)
                if n >= 3:
                    eng.wait_ge(S("w_lo"), n - 2)
                if g[0] == "gu":
                    b = g[2]
                    o, w = HD * (b % 4), IW[b]
                    for k in range(KB):
                        ins = eng.transpose(bk[:, P * k:P * k + w], src[0:w, o + P * k:o + P * k + P],
                                            ident[0:w, 0:w])
                else:
                    for k, b in enumerate(GRP[g[2]]):
                        ins = eng.transpose(bk[0:IW[b], P * k:P * k + P], src[:, P * b:P * b + IW[b]],
                                            ident[:, :])
                ins.then_inc(S("w_tr"), 1)

            def project(p, hi, lo, c):
                a, b = CH[c]
                n = 3 * KB
                i = 0
                for k in range(KB):
                    for xt, w in ((xt_hi[p], hi), (xt_hi[p], lo), (xt_lo[p], hi)):
                        ins = eng.matmul(gu[c][:, 0:b - a], xt[:, k, :], w[:, k, a:b],
                                         start=(i == 0), stop=(i == n - 1))
                        i += 1
                return ins

            def gate(t, p):
                eng.wait_ge(S("xt_lo"), t + 1)
                for c in range(NC_):
                    if isinstance(t, int) and t == 0:
                        eng.wait_ge(S("w_lo"), GRP[c][-1] + 1)
                    else:
                        eng.wait_ge(S("u_mul"), 3 * t + c - 2)
                    project(p, wg_hi, wg_lo, c).then_inc(S("g_mm"), 1)

            def up(t, p, c):
                if not is_last(t, 1):
                    eng.wait_ge(S("g_act"), 3 * t + 3 + c + 1)
                else:
                    eng.wait_ge(S("u_mul"), done("u_mul", 3 * t - 3 + c + 1))
                project(p, wu_hi, wu_lo, c).then_inc(S("u_mm"), 1)

            def h_transpose(t, g):
                eng.wait_ge(S("h_done"), done("h_done", 3 * t + g + 1))
                eng.wait_ge(S("ht_lo"), 3 * t + g + 1)
                for k, b in enumerate(GRP[g]):
                    ins = eng.transpose(tp[g][0:IW[b], P * k:P * k + P], h_buf[:, P * b:P * b + IW[b]],
                                        ident[:, :])
                ins.then_inc(S("ht_tr"), 1)

            def down(t, g, b_):
                eng.wait_ge(S("ht_lo"), done("ht_lo", 3 * t + g + 1))
                if g == 0:
                    eng.wait_ge(S("y_done"), t + 1)
                for k, b in enumerate(GRP[g]):
                    w = IW[b]
                    hi, lo = ht_hi[b_][0:w, k, :], ht_lo[b_][0:w, k, :]
                    eng.matmul(dn[:, :], hi, wd_hi[0:w, b, :], start=(b == 0), stop=False)
                    eng.matmul(dn[:, :], hi, wd_lo[0:w, b, :], start=False, stop=False)
                    ins = eng.matmul(dn[:, :], lo, wd_hi[0:w, b, :], start=False, stop=(b == IB - 1))
                ins.then_inc(S("d_mm"), 1)

            eng.wait_ge(S("consts"), 1)
            x_transpose(0, 0)
            x_transpose(1, 1)
            for n in range(N_WG):
                weights_transpose(n)
            gate(0, 0)
            for n in range(N_WG, N_ALL):
                weights_transpose(n)
            eng.wait_ge(S("w_lo"), N_ALL)

            def step_fn(t, p):
                q = 1 - p
                if not is_last(t, 1):
                    gate(t + 1, q)
                up(t, p, 0)
                eng.wait_ge(S("sel_done"), done("sel_done", t + 1))
                eng.matmul(xb[0:1, 0:1], good, one_c, start=True, stop=True).then_inc(S("flag_mm"), 1)
                up(t, p, 1)
                up(t, p, 2)
                if not is_last(t, 2):
                    x_transpose(t + 2, p)
                h_transpose(t, 0)
                h_transpose(t, 1)
                down(t, 0, p)
                h_transpose(t, 2)
                down(t, 1, q)
                down(t, 2, p)

            steps(eng, step_fn)

            def x2t_transpose(t):
                eng.wait_ge(S("x16"), t + 1)
                if 0 < t:
                    eng.wait_ge(S("x2t_ev"), t)
                if t == TH:
                    eng.wait_ge(S("vgu_ev"), MB)
                bk = t2gu[:, :].bitcast(f16)
                for j in range(2 * KB):
                    ins = eng.transpose(bk[:, P * j:P * j + P],
                                        x16[:, t * 2 * HD + P * j:t * 2 * HD + P * j + P], ident16[:, :])
                ins.then_inc(S("x2t_tr"), 1)

            def vgu_transpose(m):
                if isinstance(m, int) and m == 0:
                    eng.wait_ge(S("x2t_ev"), TH)
                else:
                    eng.wait_ge(S("vgu_ev"), m)
                bk = t2gu[:, :].bitcast(f16)
                for w, src in enumerate((ng, nu)):
                    for k in range(KB):
                        o = (w * KB + k) * P
                        ins = eng.transpose(bk[:, o:o + P],
                                            src[:, bass.ds(m, 1), P * k:P * k + P].rearrange("p a c -> p (a c)"),
                                            ident16[:, :])
                ins.then_inc(S("vgu_tr"), 1)

            def vd_transpose(m):
                if not (isinstance(m, int) and m == 0):
                    eng.wait_ge(S("vd_ev"), m)
                bk = t2d[:, :].bitcast(f16)
                for hb in range(KB):
                    ins = eng.transpose(bk[:, P * hb:P * hb + P], nd[:, hb, bass.ds(m * P, P)], ident16[:, :])
                ins.then_inc(S("vd_tr"), 1)

            def gate_up2(q, m, half):
                tok = slice(half * HALF, half * HALF + HALF)
                for w, bk in enumerate((g2, u2)):
                    if not (isinstance(q, int) and q == 0):
                        eng.wait_ge(S(("sg_done", "h2_done")[w]), q)
                    for k in range(KB):
                        for part in range(2):
                            ins = eng.matmul(bk[:, :], vgu[:, w * KB + k, bass.ds(m * P, P)],
                                             x2t[:, part, k, tok], start=(k + part == 0),
                                             stop=(k == KB - 1 and part == 1))
                    ins.then_inc(S(("g2_mm", "u2_mm")[w]), 1)

            def down2(q, m, p, first, last):
                eng.wait_ge(S("h2_lo"), q + 1)
                for j in range(TH):
                    if first and q:
                        eng.wait_ge(S("y2_done"), j + 1)
                    c = slice(P * j, P * j + P)
                    rhs = vd[:, bass.ds(m, 1), :].rearrange("p a c -> p (a c)")
                    eng.matmul(acc[j][:, :], h2_hi[p][:, c], rhs, start=first, stop=False)
                    eng.matmul(acc[j][:, :], h2_lo[p][:, c], rhs, start=False, stop=last
                               ).then_inc(S("dn_mm"), 1)

            for t in range(TH):
                x2t_transpose(t)
            loads = {0: 0, NG_SPLIT[1]: 1, NG_SPLIT[2]: 2}
            eng.wait_ge(S("n2_0"), 32)
            vgu_transpose(0)
            vgu_transpose(1)
            eng.wait_ge(S("vgu_ev"), 1)
            gate_up2(0, 0, 0)
            eng.wait_ge(S("nd"), 16)
            eng.wait_ge(S("n2_1"), 32)
            eng.wait_ge(S("y_done"), done("y_done", NT))

            def step2(q, p, more):
                first_half = in_half[0] == 0
                m = q if first_half else q - MB
                if more:
                    vgu_transpose(q + 2)
                if first_half:
                    vd_transpose(q)
                if not (isinstance(q, int) and q == 2 * MB - 1):
                    if isinstance(q, int) and q == MB - 1:
                        eng.wait_ge(S("x2t_ev"), NT)
                        gate_up2(q + 1, 0, 1)
                        in_half[0] = 1
                    else:
                        if first_half:
                            eng.wait_ge(S("vgu_ev"), q + 2)
                        gate_up2(q + 1, m + 1, 0 if first_half else 1)
                if first_half:
                    eng.wait_ge(S("vd_ev"), q + 1)
                down2(q, m, p, isinstance(q, int) and q in (0, MB),
                      isinstance(q, int) and q in (MB - 1, 2 * MB - 1))
                if isinstance(q, int) and q == 1:
                    eng.wait_ge(S("n2_2"), 32)

            in_half = [0]
            steps2(eng, step2, between=lambda: [x2t_transpose(t) for t in range(TH, NT)])


_INS = ['L0_attn_x', 'L0_attn_w_gate', 'L0_attn_w_up', 'L0_attn_w_down',
        'L0_ffn_W_gate', 'L0_ffn_W_up', 'L0_ffn_W_down']
_OUTS = [((4, 256, 512), 'float32')]


def kernel(**inputs):
    import numpy as _np
    import concourse.bacc as _bacc
    from concourse import mybir as _mybir
    from concourse.bass_utils import run_bass_kernel_spmd as _run

    nc = _bacc.Bacc("TRN2", target_bir_lowering=False, num_devices=1)
    arrays, args = {}, []
    for name in _INS:
        a = _np.ascontiguousarray(inputs[name])
        arrays[f"in_{name}_dram"] = a
        args.append(nc.dram_tensor(f"in_{name}_dram", a.shape, _mybir.dt.from_np(a.dtype), kind="ExternalInput").ap())
    for i, (shape, dtype) in enumerate(_OUTS):
        dt = _mybir.dt.from_np(_np.dtype(dtype))
        args.append(nc.dram_tensor(f"out_{i}_dram", shape, dt, kind="ExternalOutput").ap())
    build(nc, *args)
    r = _run(nc, [arrays], core_ids=[0])
    return r.results[0]["out_0_dram"]
```

```python
import concourse.bass as bass
from concourse import mybir
from contextlib import ExitStack


def build(nc, x, w_gate, w_up, w_down, v_gate, v_up, v_down, out):
    f32, f32r = mybir.dt.float32, mybir.dt.float32r
    f16, i32, i8 = mybir.dt.float16, mybir.dt.int32, mybir.dt.int8
    ALU, ACT = mybir.AluOpType, mybir.ActivationFunctionType

    P = 128
    HD = x.shape[2]
    TOK = x.shape[0] * x.shape[1]
    NT = TOK // P
    KB = HD // P
    I = w_gate.shape[0]
    IB = -(-I // P)
    IW = [min(P, I - P * b) for b in range(IB)]
    CH = [(c, min(c + 512, I)) for c in range(0, I, 512)]
    NC_ = len(CH)
    GRP = [list(range(4 * g, min(4 * g + 4, IB))) for g in range(NC_)]
    ZERO = I // 2
    M2 = v_gate.shape[0]
    MB = M2 // P
    HALF = TOK // 2
    TH = HALF // P
    LAST = 2 * MB - 4
    UP = 1024.0
    EPS = 1e-5
    START, SLOPE, AIM, NEAR = 0.782, 655.0, ZERO + 8, 7.5
    PASSES = 4

    xf = x.rearrange("b s h -> (b s) h")
    of = out.rearrange("b s h -> (b s) h")
    x2_dram = nc.dram_tensor("x2_scratch", [TOK, HD], f32).ap()

    ctx = ExitStack()
    with ctx:
        base = -(-nc.sbuf_base // 64) * 64
        at = [base]

        def place(name, shape, dt, size, offset=None):
            if offset is None:
                offset = at[0]
                at[0] += -(-size // 32) * 32
            return nc.alloc_sbuf_tensor_at(name, [P] + shape, dt, offset=offset), offset

        wg_hi, A0 = place("wg_hi", [KB, I], f32r, KB * I * 4)
        wg_lo, _ = place("wg_lo", [KB, I], f32r, KB * I * 4)
        wu_hi, B0 = place("wu_hi", [KB, I], f32r, KB * I * 4)
        wu_lo, _ = place("wu_lo", [KB, I], f32r, KB * I * 4)
        wd_hi, C0 = place("wd_hi", [IB, HD], f32r, IB * HD * 4)
        wd_lo, _ = place("wd_lo", [IB, HD], f32r, IB * HD * 4)
        x16, X0 = place("x16", [NT * 2 * HD], f16, NT * 2 * HD * 2)
        nat = [place("nat0", [2048], f32, 0, X0)[0], place("nat1", [2048], f32, 0, X0 + 8192)[0]]
        x_in0, XI0 = place("x_in0", [HD], f32, HD * 4)
        x_in1, _ = place("x_in1", [HD], f32, HD * 4)
        x_in = [x_in0, x_in1]
        x_res, _ = place("x_res", [HD], f32, HD * 4)
        x2, _ = place("x2", [HD], f32, HD * 4)
        xt_hi0, XT0 = place("xt_hi0", [KB, P], f32r, HD * 4)
        xt_lo0, _ = place("xt_lo0", [KB, P], f32r, HD * 4)
        xt_hi1, _ = place("xt_hi1", [KB, P], f32r, HD * 4)
        xt_lo1, _ = place("xt_lo1", [KB, P], f32r, HD * 4)
        xt_hi, xt_lo = [xt_hi0, xt_hi1], [xt_lo0, xt_lo1]
        s0, S0 = place("s0", [I], f32, I * 4)
        a0, _ = place("a0", [I], f32, I * 4)
        s1, _ = place("s1", [I], f32, I * 4)
        a1, _ = place("a1", [I], f32, I * 4)
        s_buf, a_buf = [s0, s1], [a0, a1]
        h_buf, _ = place("h_buf", [I], f32, I * 4)
        ht_hi = [place(f"ht_hi{i}", [4, P], f32r, 2048)[0] for i in range(2)]
        ht_lo = [place(f"ht_lo{i}", [4, P], f32r, 2048)[0] for i in range(2)]
        signs, _ = place("signs", [I], i8, I)
        ident, _ = place("ident", [P], f32, P * 4)
        ident16, _ = place("ident16", [P], f16, P * 2)
        rank, _ = place("rank", [17], f32, 17 * 4)
        top, _ = place("top", [16], f32, 64)
        small, _ = place("small", [64], f32, 256)
        ints, _ = place("ints", [8], i32, 32)
        nat2, N2 = place("nat2", [2048], f32, 8192)
        nat.append(nat2)
        assert at[0] <= nc.sbuf_usable_end, (at[0], nc.sbuf_usable_end)
        ng, _ = place("ng", [MB, HD], f16, 0, A0)
        nu, _ = place("nu", [MB, HD], f16, 0, A0 + MB * HD * 2)
        nd, _ = place("nd", [KB, M2], f16, 0, A0 + 2 * MB * HD * 2)
        vgu, _ = place("vgu", [2 * KB, M2], f16, 0, B0)
        res = [place(f"res{j}", [HD], f32, 0, B0 + 2 * KB * M2 * 2 + j * HD * 4)[0] for j in range(TH)]
        vd, _ = place("vd", [MB, HD], f32r, 0, C0)
        C1 = C0 + MB * HD * 4
        h2_hi = [place(f"h2_hi{i}", [HALF], f32r, 0, C1 + i * 2048)[0] for i in range(4)]
        h2_lo = [place(f"h2_lo{i}", [HALF], f32r, 0, C1 + 8192 + i * 2048)[0] for i in range(4)]
        sg = [place(f"sg{i}", [HALF], f32, 0, XI0 + i * 2048)[0] for i in range(2)]
        h2 = [place(f"h2{i}", [HALF], f32, 0, XT0 + i * 2048)[0] for i in range(2)]
        x2t = [place("x2t_hi", [KB, TOK], f16, 0, N2)[0], place("x2t_lo", [KB, TOK], f16, 0, S0)[0]]

        cols = iter(range(64))

        def col(n=1):
            c = [next(cols) for _ in range(n)]
            return small[:, c[0]:c[-1] + 1]

        half_c, one_c, good, keep, below, cnt, jj, jok = (col() for _ in range(8))
        abs_sum, sign_sum, err, far, step, neg_t, unit, unit2 = (col() for _ in range(8))
        start_c, unit_c, unit2_c, aim_c, minus_c = (col() for _ in range(5))
        pos_t = [col(), col()]
        stats, mv, rstd, var_e = col(6), col(2), col(), col()
        stats2, mv2, rstd2, var_e2 = col(6), [col(2) for _ in range(TH)], col(TH), col(TH)
        tie_m, le = col(), col()
        bit, found, tried, gain, n_good = (ints[:, i:i + 1] for i in range(5))

        def bank(name):
            return ctx.enter_context(nc.psum_tensor(name, [P, 512], f32))

        gu = [bank(f"gu{i}") for i in range(3)]
        tp = [bank(f"tp{i}") for i in range(3)]
        dn = bank("dn")
        xb = bank("xb")
        g2, u2, t2gu, t2d = gu[0], gu[1], xb, gu[2]
        acc = [tp[0], tp[1], tp[2], dn]

        def x2t_bank(t):
            return tp[1 + t % 2] if t < 4 else t2gu


        sem = {}

        def S(name):
            if name not in sem:
                sem[name] = ctx.enter_context(nc.semaphore(name))
            return sem[name]

        CR = {"sel_done": 1, "y_done": 1, "ht_lo": 3, "d_mm": 2, "x2_saved": 16}

        def done(name, n):
            return n + CR.get(name, 0)

        TURNS = NT - 2

        def turns(eng, body):
            with eng.Fori(0, TURNS - 1, 2) as i:
                body(i, 0)
                body(i + 1, 1)

        def prologue():
            n = 5
            for k in range(n):
                yield ("w", k)
            yield ("x", 0)
            yield ("x", 1)
            for kind, t in (("g", 0), ("g", 1), ("u", 0)):
                for c in range(NC_):
                    for k in range(KB):
                        yield ("mm", kind, t, c, k)
                        if n < N_ALL:
                            yield ("w", n)
                            n += 1
            assert n == N_ALL

        def steps2(eng, fn, halfway=lambda: None):
            for q in range(2):
                fn(q, q % 2, 0)
            with eng.Fori(2, MB - 3, 2) as i:
                fn(i, 0, 0)
                fn(i + 1, 1, 0)
            fn(MB - 2, 0, 0)
            fn(MB - 1, 1, 0)
            halfway()
            for q in range(2):
                fn(MB + q, q, 1)
            with eng.Fori(MB + 2, LAST - 1, 2) as i:
                fn(i, 0, 1)
                fn(i + 1, 1, 1)
            for q in range(LAST, 2 * MB):
                fn(q, q % 2, 1)

        def nat_rows(src, b):
            return src[P * b:P * b + IW[b], :]

        NSLAB = 10

        def slab_view(n):
            return nat[n % 3]

        def prologue_groups():
            for w in range(2):
                for b in range(IB):
                    yield ("gu", w, b)
            for hb in range(KB):
                for g in range(NC_):
                    yield ("d", hb, g)

        GROUPS = list(prologue_groups())
        N_WG, N_WU, N_ALL = IB, 2 * IB, len(GROUPS)

        def slab_of(g):
            return 3 * g[1] + g[2] // 4 if g[0] == "gu" else 6 + g[1]

        last_group_of_slab = {slab_of(g): n for n, g in enumerate(GROUPS)}

        def group_dst(g):
            n = GROUPS.index(g)
            if g[0] == "gu":
                hi, lo = ((wg_hi, wg_lo), (wu_hi, wu_lo))[g[1]]
                b = g[2]
                c = slice(P * b, P * b + IW[b])
                src = tp[n % 3][:, :].rearrange("p (k c) -> p k c", k=KB)[:, :, 0:IW[b]]
                return hi[:, :, c], lo[:, :, c], src
            bl = GRP[g[2]]
            c = slice(P * g[1], P * g[1] + P)
            src = tp[n % 3][:, 0:P * len(bl)].rearrange("p (k c) -> p k c", c=P)
            return wd_hi[:, bl[0]:bl[-1] + 1, c], wd_lo[:, bl[0]:bl[-1] + 1, c], src

        def slot(q, p):
            return q - LAST if isinstance(q, int) and q >= LAST else p

        X2T_AT = {0: (TH,), 1: (TH + 1,), MB - 2: (TH + 2, TH + 3)}
        vg_v = v_gate.rearrange("(m p) h -> p m h", p=P)
        vu_v = v_up.rearrange("(m p) h -> p m h", p=P)
        vd_v = v_down.rearrange("(b p) m -> p b m", p=P)
        NG_SPLIT = [0, 2, 7, MB]
        block = ctx.enter_context(nc.Block())

        @block.sync
        def _(eng):
            eng.nop().then_inc(S("x2_saved"), 16)
            for n in range(NSLAB):
                if n >= 3:
                    eng.wait_ge(S("w_tr"), last_group_of_slab[n - 3] + 1)
                dst, s = slab_view(n), S(f"slab{n}")
                if n < 6:
                    src = (w_gate, w_up)[n // 3]
                    bl = GRP[n % 3]
                    full = [b for b in bl if IW[b] == P]
                    if n == 0:
                        eng.dma_start(dst[:, 0:HD], nat_rows(src, 0)).then_inc(S("first"), 16)
                        eng.dma_start(dst[:, HD:4 * HD].rearrange("p (b h) -> p b h", h=HD),
                                      src[P:4 * P, :].rearrange("(b p) h -> p b h", p=P)).then_inc(s, 16)
                        continue
                    eng.dma_start(dst[:, 0:HD * len(full)].rearrange("p (b h) -> p b h", h=HD),
                                  src[P * full[0]:P * full[-1] + P, :].rearrange("(b p) h -> p b h", p=P)
                                  ).then_inc(s, 16)
                    for b in bl[len(full):]:
                        o = HD * (b - bl[0])
                        eng.dma_start(dst[0:IW[b], o:o + HD], nat_rows(src, b)).then_inc(s, 16)
                else:
                    hb = n - NC_ * 2
                    eng.dma_start(dst[:, 0:I], w_down[P * hb:P * hb + P, :]).then_inc(s, 16)

            def load_next(t, p):
                eng.wait_ge(S("x_tr"), t + 1)
                eng.wait_ge(S("x_loaded"), 16 * t + 32)
                eng.dma_start(x_in[p][:, :], xf[bass.ds(t * P + 2 * P, P), :]).then_inc(S("x_loaded"), 16)

            def load_residual(t):
                eng.wait_ge(S("y_done"), t + 1)
                eng.dma_start(x_res[:, :], xf[bass.ds(t * P, P), :]).then_inc(S("xr_loaded"), 16)

            def save_x2(t):
                eng.wait_ge(S("x2_done"), t + 1)
                eng.dma_start(x2_dram[bass.ds(t * P, P), :], x2[:, :]).then_inc(S("x2_saved"), 16)

            def turn(t, p, more=True):
                load_residual(t)
                if more:
                    load_next(t + 1, 1 - p)
                save_x2(t)

            load_next(0, 0)
            with eng.Fori(0, TURNS - 3, 2) as i:
                turn(i, 0)
                turn(i + 1, 1)
            turn(TURNS - 2, 0)
            turn(TURNS - 1, 1, more=False)
            load_residual(NT - 2)
            eng.wait_ge(S("g_mm"), 3 * NT)
            for n, (lo, hi) in enumerate(zip(NG_SPLIT, NG_SPLIT[1:])):
                eng.dma_start(ng[:, lo:hi, :], vg_v[:, lo:hi, :]).then_inc(S(f"n2_{n}"), 16)
                eng.dma_start(nu[:, lo:hi, :], vu_v[:, lo:hi, :]).then_inc(S(f"n2_{n}"), 16)
                if n == 0:
                    eng.dma_start(nd[:, :, :], vd_v).then_inc(S("nd"), 16)
            save_x2(NT - 2)
            load_residual(NT - 1)
            save_x2(NT - 1)
            eng.wait_ge(S("x2_saved"), 16 * (NT + 1))
            eng.wait_ge(S("u_mm"), 3 * NT)
            for j in range(TH):
                eng.dma_start(res[j][:, :], x2_dram[P * j:P * j + P, :]).then_inc(S("res"), 16)
            for half in range(2):
                for j in range(TH):
                    t = TH * half + j
                    eng.wait_ge(S("o_done"), t + 1)
                    eng.dma_start(of[P * t:P * t + P, :], res[j][:, :]).then_inc(S("out"), 16)
                if half == 0:
                    eng.wait_ge(S("out"), 16 * TH)
                    for j in range(TH):
                        t = TH + j
                        eng.dma_start(res[j][:, :], x2_dram[P * t:P * t + P, :]).then_inc(S("res"), 16)
            eng.wait_ge(S("out"), 16 * NT)

        @block.gpsimd
        def _(eng):
            eng.memset(ident[:, :], 0.0)
            eng.memset(ident16[:, :], 0.0)
            eng.memset(half_c, -0.5)
            eng.memset(one_c, 1.0)
            eng.memset(minus_c, -1.0)
            eng.memset(start_c, -START / I)
            eng.memset(unit_c, -0.5 * START / I / SLOPE)
            eng.memset(unit2_c, -0.5 * 0.85 * START / I / SLOPE)
            eng.memset(aim_c, float(I - 2 * AIM))
            for k in range(17):
                eng.memset(rank[:, k:k + 1], float(k - 1))
            eng.drain()
            for m in (ident, ident16):
                eng.affine_select(out=m[:, :], in_=m[:, :], compare_op=ALU.not_equal, fill=1.0,
                                  base=0, pattern=[[-1, P]], channel_multiplier=1)
            eng.drain()
            eng.nop().then_inc(S("consts"), 1)

            def search_start(t):
                eng.wait_ge(S("abs_done"), t + 1)
                eng.tensor_tensor(unit, abs_sum, unit_c, ALU.mult)
                eng.tensor_tensor(unit2, abs_sum, unit2_c, ALU.mult)
                eng.tensor_tensor(neg_t, abs_sum, start_c, ALU.mult).then_inc(S("thr"), 1)
                eng.drain()

            def rstd_of(t):
                eng.wait_ge(S("var_done"), t + 1)
                eng.tensor_tensor(rstd, var_e, half_c, ALU.pow).then_inc(S("rstd"), 1)

            def search_moves(t, passes, p, reused):
                for n in passes:
                    eng.wait_ge(S("counted"), t * PASSES + n + 1)
                    eng.tensor_tensor(err, sign_sum, aim_c, ALU.subtract)
                    eng.drain()
                    eng.tensor_scalar(far, err, err, 4 * NEAR * NEAR, ALU.mult, ALU.is_gt)
                    eng.tensor_scalar(step, err, unit if n < 2 else unit2, None, ALU.mult)
                    eng.drain()
                    last = n == PASSES - 1
                    ins = eng.tensor_scalar(neg_t, step, far, neg_t, ALU.mult, ALU.add)
                    if last:
                        eng.drain()
                        if reused:
                            eng.wait_ge(S("sel_done"), t)
                        ins = eng.tensor_tensor(pos_t[p], neg_t, minus_c, ALU.mult)
                    ins.then_inc(S("thr"), 1)
                    eng.drain()

            search_start(0)
            search_moves(0, range(PASSES), 0, False)
            search_start(1)
            search_moves(1, range(2), 1, False)

            def turn(t, p, more=True):
                search_moves(t + 1, range(2, PASSES), 1 - p, True)
                if more:
                    search_start(t + 2)
                    search_moves(t + 2, range(2), p, True)
                rstd_of(t)

            turns(eng, turn)
            turn(NT - 2, 0, more=False)
            rstd_of(NT - 1)
            for t in range(NT):
                eng.wait_ge(S("var2_done"), t + 1)
                j = t % TH
                eng.tensor_tensor(rstd2[:, j:j + 1], var_e2[:, j:j + 1], half_c, ALU.pow).then_inc(S("rstd2"), 1)

        @block.scalar
        def _(eng):
            def x_hi(t, p):
                eng.wait_ge(S("x_tr"), t + 1)
                eng.activation(xt_hi[p][:, :, :], xb[:, :].rearrange("p (k c) -> p k c", k=KB),
                               ACT.Copy).then_inc(S("xt_hi"), 1)

            def weights_hi(n):
                hi, _, src = group_dst(GROUPS[n])
                eng.wait_ge(S("w_tr"), n + 1)
                eng.activation(hi, src, ACT.Copy).then_inc(S("w_hi"), 1)

            def silu(t, p, c):
                lo, hi = CH[c]
                eng.wait_ge(S("g_mm"), 3 * t + c + 1)
                eng.activation(s_buf[p][:, lo:hi], gu[c][:, 0:hi - lo], ACT.Silu).then_inc(S("g_act"), 1)

            def absolute(t, p):
                eng.wait_ge(S("g_act"), 3 * t + 3)
                eng.activation(a_buf[p][:, :], s_buf[p][:, :], ACT.Abs,
                               accum_out=abs_sum).then_inc(S("abs_done"), 1)

            def count(t, p, n):
                eng.wait_ge(S("thr"), t * (PASSES + 1) + n + 1)
                eng.wait_ge(S("abs_done"), t + 1)
                eng.activation(signs[:, :], a_buf[p][:, :], ACT.Sign, bias=neg_t,
                               accum_out=sign_sum).then_inc(S("counted"), 1)

            def h_hi(t, g, b):
                eng.wait_ge(S("ht_tr"), 3 * t + g + 1)
                eng.wait_ge(S("d_mm"), 3 * t + g + 1)
                w = P * len(GRP[g])
                eng.activation(ht_hi[b][:, 0:len(GRP[g]), :],
                               tp[g][:, 0:w].rearrange("p (k c) -> p k c", c=P),
                               ACT.Copy).then_inc(S("ht_hi"), 1)

            for t in range(2):
                eng.dma_start(x_in[t][:, :], xf[P * t:P * t + P, :]).then_inc(S("x_loaded"), 16)
            counts = {("g", 1, 1): (0, 0), ("g", 1, 3): (0, 1), ("g", 1, 6): (0, 2), ("g", 1, 8): (0, 3),
                      ("u", 0, 4): (1, 0), ("u", 0, 8): (1, 1)}
            for e in prologue():
                if e[0] == "w":
                    weights_hi(e[1])
                elif e[0] == "x":
                    x_hi(e[1], e[1])
                else:
                    _, kind, t, c, k = e
                    if kind == "g" and k == KB - 1:
                        silu(t, t, c)
                        if c == NC_ - 1:
                            absolute(t, t)
                    if (kind, t, KB * c + k) in counts:
                        tile, n = counts[kind, t, KB * c + k]
                        count(tile, tile, n)
            h_hi(0, 0, 0)

            def turn(t, p, more=True):
                q = 1 - p
                if more:
                    eng.wait_ge(S("u_mm"), 3 * t + 3)
                    x_hi(t + 2, p)
                h_hi(t, 1, q)
                count(t + 1, q, 2)
                h_hi(t, 2, p)
                count(t + 1, q, 3)
                if more:
                    eng.wait_ge(S("h_done"), 3 * t + 3)
                    for c in range(NC_):
                        silu(t + 2, p, c)
                    absolute(t + 2, p)
                    count(t + 2, p, 0)
                    h_hi(t + 1, 0, q)
                    count(t + 2, p, 1)

            turns(eng, turn)
            turn(NT - 2, 0, more=False)

            def x2t_copy(t):
                eng.wait_ge(S("x2t_tr"), t + 1)
                src = x2t_bank(t)[:, :].bitcast(f16).rearrange("p (a k c) -> p a k c", a=2, c=P)
                for part in range(2):
                    ins = eng.activation(x2t[part][:, :, P * t:P * t + P], src[:, part], ACT.Copy)
                ins.then_inc(S("x2t_ev"), 1)

            def vgu_copy(m):
                eng.wait_ge(S("vgu_tr"), m + 1)
                src = t2gu[:, :].bitcast(f16).rearrange("p (j c) -> p j c", c=P)
                eng.activation(vgu[:, :, bass.ds(m * P, P)], src, ACT.Copy).then_inc(S("vgu_ev"), 1)

            def gate2(q, p):
                eng.wait_ge(S("g2_mm"), q + 1)
                if not (isinstance(q, int) and q < 2):
                    eng.wait_ge(S("h2_done"), q - 1)
                eng.activation(sg[p][:, :], g2[:, :], ACT.Silu, scale=1.0 / UP).then_inc(S("sg_done"), 1)

            def h2_high(q, p):
                eng.wait_ge(S("h2_done"), q + 1)
                if not (isinstance(q, int) and (q < 2 or q >= LAST + 2)):
                    eng.wait_ge(S("dn_mm"), 4 * q - 4)
                eng.activation(h2_hi[slot(q, p)][:, :], h2[p][:, :], ACT.Copy).then_inc(S("h2_hi"), 1)

            eng.wait_ge(S("h_done"), 3 * (NT - 1))
            for t in range(TH - 1):
                x2t_copy(t)
            eng.wait_ge(S("u_mm"), 3 * NT)
            vgu_copy(0)
            x2t_copy(TH - 1)
            gate2(0, 0)
            vgu_copy(1)
            for g in range(NC_):
                h_hi(NT - 1, g, (NT - 1 + g) % 2)
            eng.wait_ge(S("d_mm"), done("d_mm", 3 * NT))

            def step2(q, p, half):
                if not (isinstance(q, int) and q == 0):
                    gate2(q, p)
                if half == 0 and not (isinstance(q, int) and q >= MB - 2):
                    vgu_copy(q + 2)
                at = X2T_AT.get(q, ()) if isinstance(q, int) else ()
                if len(at) == 2:
                    x2t_copy(at[0])
                h2_high(q, p)
                if at:
                    x2t_copy(at[-1])

            steps2(eng, step2)

        @block.vector
        def _(eng):
            v = nc.vector
            for name, n in CR.items():
                if name in ("sel_done", "y_done", "ht_lo"):
                    eng.nop().then_inc(S(name), n)

            def x_low(t, p):
                eng.wait_ge(S("xt_hi"), t + 1)
                v.tensor_tensor(xt_lo[p][:, :, :], xb[:, :].rearrange("p (k c) -> p k c", k=KB),
                                xt_hi[p][:, :, :], ALU.subtract).then_inc(S("xt_lo"), 1)

            def weights_lo(n):
                hi, lo, src = group_dst(GROUPS[n])
                eng.wait_ge(S("w_hi"), n + 1)
                v.tensor_tensor(lo, src, hi, ALU.subtract).then_inc(S("w_lo"), 1)

            def select(t, p, part=None):
                a = a_buf[p]
                if part in (None, 0):
                    eng.wait_ge(S("thr"), t * (PASSES + 1) + PASSES + 1)
                    eng.wait_ge(S("abs_done"), t + 1)
                    v.tensor_scalar(h_buf[:, :], a[:, :], pos_t[p], None, ALU.is_lt, ALU.add, accum_out=cnt)
                    eng.drain()
                if part in (None, 1):
                    v.scalar_tensor_tensor(h_buf[:, :], a[:, :], pos_t[p], a[:, :], ALU.is_lt, ALU.mult)
                    eng.drain()
                if part in (None, 2):
                    v.tensor_scalar(jj, cnt, float(ZERO + 1), None, ALU.subtract)
                    v.max(top[:, 0:8], h_buf[:, :])
                    eng.drain()
                if part in (None, 3):
                    v.tensor_scalar(jok, jj, 14.5, None, ALU.is_le)
                    v.match_replace(h_buf[:, :], top[:, 0:8], h_buf[:, :], -1.0)
                    eng.drain()
                if part in (None, 4):
                    v.max(top[:, 8:16], h_buf[:, :])
                    eng.drain()
                    v.scalar_tensor_tensor(h_buf[:, 0:16], rank[:, 1:17], jj, top[:, :], ALU.is_equal,
                                           ALU.mult, accum_out=keep)
                    v.scalar_tensor_tensor(h_buf[:, 16:32], rank[:, 0:16], jj, top[:, :], ALU.is_equal,
                                           ALU.mult, accum_out=below)
                    eng.drain()
                    v.tensor_scalar(good, keep, below, jok, ALU.is_gt, ALU.mult).then_inc(S("sel_done"), 1)

            def up_times_s(t, p, c):
                lo, hi = CH[c]
                eng.wait_ge(S("u_mm"), 3 * t + c + 1)
                eng.wait_ge(S("abs_done"), t + 1)
                v.tensor_tensor(s_buf[p][:, lo:hi], gu[c][:, 0:hi - lo], s_buf[p][:, lo:hi],
                                ALU.mult).then_inc(S("u_mul"), 1)

            def settle(t, p):
                a, found_f = a_buf[p], found.bitcast(f32)
                eng.wait_ge(S("flag_mm"), t + 1)
                bk = tp[0] if isinstance(t, int) and t == NT - 1 else xb
                v.tensor_copy(n_good[0:1, :], bk[0:1, 0:1]).then_inc(S("flag_read"), 1)
                eng.drain()
                n = eng.value_load(n_good[0:1, :], min_val=0, max_val=P)
                with eng.If(n != P):
                    v.memset(bit.bitcast(f32), 2.0)
                    v.memset(found, 0)
                    eng.drain()
                    with eng.Fori(0, 31):
                        v.tensor_tensor(tried, found, bit, ALU.bitwise_or)
                        eng.drain()
                        v.tensor_scalar(h_buf[:, :], a[:, :], tried.bitcast(f32), None, ALU.is_lt,
                                        ALU.add, accum_out=cnt)
                        eng.drain()
                        v.tensor_scalar(le, cnt, ZERO - 0.5, None, ALU.is_le)
                        eng.drain()
                        v.tensor_scalar(gain, bit, le, None, ALU.mult)
                        eng.drain()
                        v.tensor_tensor(found, found, gain, ALU.bitwise_or)
                        v.tensor_scalar(bit, bit, 1, None, ALU.logical_shift_right)
                        eng.drain()
                    v.tensor_scalar(h_buf[:, :], a[:, :], found_f, None, ALU.is_lt, ALU.add, accum_out=cnt)
                    eng.drain()
                    v.tensor_scalar(tie_m, cnt, -1.0, float(ZERO), ALU.mult, ALU.add)
                    v.tensor_scalar(h_buf[:, :], a[:, :], found_f, None, ALU.is_equal)
                    eng.drain()
                    v.tensor_tensor_scan(h_buf[:, :], h_buf[:, :], h_buf[:, :], 0.0, ALU.add, ALU.max)
                    eng.drain()
                    v.tensor_scalar(h_buf[:, :], h_buf[:, :], tie_m, None, ALU.is_le)
                    eng.drain()
                    v.scalar_tensor_tensor(h_buf[:, :], a[:, :], found_f, h_buf[:, :], ALU.is_equal, ALU.mult)
                    eng.drain()
                    v.scalar_tensor_tensor(a[:, :], h_buf[:, :], -3e38, a[:, :], ALU.mult, ALU.add)
                    v.tensor_copy(keep, found_f)
                    eng.drain()
                with eng.Else():
                    eng.nop()
                eng.drain()

            def hidden(t, p, c):
                lo, hi = CH[c]
                v.scalar_tensor_tensor(h_buf[:, lo:hi], a_buf[p][:, lo:hi], keep, s_buf[p][:, lo:hi],
                                       ALU.is_ge, ALU.mult).then_inc(S("h_done"), 1)

            def h_low(t, g, b):
                eng.wait_ge(S("ht_hi"), 3 * t + g + 1)
                w, n = P * len(GRP[g]), len(GRP[g])
                v.tensor_tensor(ht_lo[b][:, 0:n, :], tp[g][:, 0:w].rearrange("p (k c) -> p k c", c=P),
                                ht_hi[b][:, 0:n, :], ALU.subtract).then_inc(S("ht_lo"), 1)

            def residual_add(t):
                eng.wait_ge(S("d_mm"), done("d_mm", 3 * t + 3))
                eng.wait_ge(S("xr_loaded"), 16 * t + 16)
                eng.wait_ge(S("x2_saved"), 16 * t + 16)
                v.tensor_tensor(x2[:, :], dn[:, :], x_res[:, :], ALU.add).then_inc(S("y_done"), 1)

            def mean_variance(t):
                eng.drain()
                v.bn_stats(stats, x2[:, :])
                eng.drain()
                v.bn_aggr(mv, stats)
                eng.drain()
                v.tensor_scalar(var_e, mv[:, 1:2], EPS, None, ALU.add).then_inc(S("var_done"), 1)

            def norm(t):
                eng.wait_ge(S("rstd"), t + 1)
                v.tensor_scalar(x2[:, :], x2[:, :], mv[:, 0:1], rstd, ALU.subtract, ALU.mult
                                ).then_inc(S("x2_done"), 1)
                eng.drain()
                hi = x16[:, bass.ds(t * 2 * HD, HD)]
                lo = x16[:, bass.ds(t * 2 * HD + HD, HD)]
                v.tensor_scalar(hi, x2[:, :], UP, None, ALU.mult)
                eng.drain()
                v.scalar_tensor_tensor(lo, x2[:, :], UP, hi, ALU.mult, ALU.subtract).then_inc(S("x16"), 1)

            parts = {("g", 1, 9): 0, ("g", 1, 11): 1, ("u", 0, 1): 2, ("u", 0, 3): 3, ("u", 0, 5): 4}
            for e in prologue():
                if e == ("mm", "g", 1, 0, 0):
                    eng.wait_ge(S("consts"), 1)
                if e[0] == "w":
                    weights_lo(e[1])
                elif e[0] == "x":
                    x_low(e[1], e[1])
                else:
                    _, kind, t, c, k = e
                    if (kind, t, KB * c + k) in parts:
                        select(0, 0, parts[kind, t, KB * c + k])
                    if kind == "u" and k == KB - 1:
                        up_times_s(0, 0, c)
            settle(0, 0)
            hidden(0, 0, 0)
            hidden(0, 0, 1)
            hidden(0, 0, 2)
            h_low(0, 0, 0)

            def turn(t, p, more=True, first=False):
                q = 1 - p
                if more:
                    x_low(t + 2, p)
                h_low(t, 1, q)
                h_low(t, 2, p)
                if not first:
                    norm(t - 1)
                select(t + 1, q)
                up_times_s(t + 1, q, 0)
                if more:
                    settle(t + 1, q)
                    hidden(t + 1, q, 0)
                up_times_s(t + 1, q, 1)
                if more:
                    eng.drain()
                    hidden(t + 1, q, 1)
                    residual_add(t)
                    h_low(t + 1, 0, q)
                up_times_s(t + 1, q, 2)
                if more:
                    mean_variance(t)
                    eng.drain()
                    hidden(t + 1, q, 2)

            turn(0, 0, first=True)
            with eng.Fori(1, TURNS - 2, 2) as i:
                turn(i, 1)
                turn(i + 1, 0)
            turn(TURNS - 1, 1)
            turn(NT - 2, 0, more=False)
            settle(NT - 1, 1)
            for c in range(NC_):
                hidden(NT - 1, 1, c)
            residual_add(NT - 2)
            mean_variance(NT - 2)
            norm(NT - 2)

            def vd_copy(m):
                eng.wait_ge(S("vd_tr"), m + 1)
                v.tensor_copy(vd[:, bass.ds(m, 1), :].rearrange("p a c -> p (a c)"),
                              t2d[:, 0:HD // 2].bitcast(f16)).then_inc(S("vd_ev"), 1)

            def h2_mul(q, p):
                eng.wait_ge(S("sg_done"), q + 1)
                eng.wait_ge(S("u2_mm"), q + 1)
                if not (isinstance(q, int) and q < 2):
                    eng.wait_ge(S("h2_hi"), q - 1)
                v.scalar_tensor_tensor(h2[p][:, :], u2[:, :], 1.0 / UP, sg[p][:, :], ALU.mult,
                                       ALU.mult).then_inc(S("h2_done"), 1)

            def h2_low(q, p):
                eng.wait_ge(S("h2_hi"), q + 1)
                n = slot(q, p)
                v.tensor_tensor(h2_lo[n][:, :], h2[p][:, :], h2_hi[n][:, :],
                                ALU.subtract).then_inc(S("h2_lo"), 1)

            h2_mul(0, 0)
            for g in range(NC_):
                h_low(NT - 1, g, (NT - 1 + g) % 2)
            residual_add(NT - 1)
            mean_variance(NT - 1)
            norm(NT - 1)

            def step2(q, p, half):
                at_ = q if isinstance(q, int) else None
                if half == 0:
                    vd_copy(q)
                if at_ != 0:
                    h2_mul(q, p)
                h2_low(q, p)
                if at_ in (MB, MB + 1):
                    for j in ((0, 1), (2, 3))[at_ - MB]:
                        statistics(j)
                    if at_ == MB + 1:
                        for j in range(TH):
                            normalise(0, j)

            def residual(half, j):
                if half == 0:
                    n = TH * MB - TH + j + 1
                else:
                    n = TH * LAST + (7, 8, 12, 16)[j]
                eng.wait_ge(S("dn_mm"), n)
                if j == 0:
                    eng.wait_ge(S("res"), 16 * TH * (half + 1))
                v.tensor_tensor(res[j][:, :], acc[j][:, :], res[j][:, :], ALU.add).then_inc(S("y2_done"), 1)

            def statistics(j):
                eng.drain()
                v.bn_stats(stats2, res[j][:, :])
                eng.drain()
                v.bn_aggr(mv2[j], stats2)
                eng.drain()
                v.tensor_scalar(var_e2[:, j:j + 1], mv2[j][:, 1:2], EPS, None, ALU.add
                                ).then_inc(S("var2_done"), 1)

            def normalise(half, j):
                eng.wait_ge(S("rstd2"), TH * half + j + 1)
                v.tensor_scalar(res[j][:, :], res[j][:, :], mv2[j][:, 0:1], rstd2[:, j:j + 1],
                                ALU.subtract, ALU.mult).then_inc(S("o_done"), 1)

            steps2(eng, step2, halfway=lambda: [residual(0, j) for j in range(TH)])
            for j in range(TH):
                residual(1, j)
                statistics(j)
                if j:
                    normalise(1, j - 1)
            normalise(1, TH - 1)

        @block.tensor
        def _(eng):
            eng.nop().then_inc(S("d_mm"), CR["d_mm"])

            def x_transpose(t, p):
                if isinstance(t, int) and t < 2:
                    eng.wait_ge(S("x_loaded"), 32)
                    if t:
                        eng.wait_ge(S("xt_lo"), t)
                else:
                    eng.wait_ge(S("x_loaded"), 16 * t + 16)
                    eng.wait_ge(S("flag_read"), t - 1)
                for k in range(KB):
                    ins = eng.transpose(xb[:, P * k:P * k + P], x_in[p][:, P * k:P * k + P], ident[:, :])
                ins.then_inc(S("x_tr"), 1)

            def weights_transpose(n):
                g = GROUPS[n]
                s = slab_of(g)
                src, bk = slab_view(s), tp[n % 3]
                if n == 0:
                    eng.wait_ge(S("first"), 16)
                else:
                    eng.wait_ge(S(f"slab{s}"), 32 if s < 6 and s % 3 == 2 else 16)
                if n >= 3:
                    eng.wait_ge(S("w_lo"), n - 2)
                if g[0] == "gu":
                    b = g[2]
                    o, w = HD * (b % 4), IW[b]
                    for k in range(KB):
                        ins = eng.transpose(bk[:, P * k:P * k + w], src[0:w, o + P * k:o + P * k + P],
                                            ident[0:w, 0:w])
                else:
                    for k, b in enumerate(GRP[g[2]]):
                        ins = eng.transpose(bk[0:IW[b], P * k:P * k + P], src[:, P * b:P * b + IW[b]],
                                            ident[:, :])
                ins.then_inc(S("w_tr"), 1)

            def project(p, hi, lo, c, k):
                a, b = CH[c]
                for i, (xt, w) in enumerate(((xt_hi[p], hi), (xt_hi[p], lo), (xt_lo[p], hi))):
                    ins = eng.matmul(gu[c][:, 0:b - a], xt[:, k, :], w[:, k, a:b],
                                     start=(k == 0 and i == 0), stop=(k == KB - 1 and i == 2))
                return ins

            def gate_block(t, p, c, k):
                if k == 0:
                    if isinstance(t, int) and t < 2:
                        if t == 0:
                            eng.wait_ge(S("w_lo"), GRP[c][-1] + 1)
                        else:
                            eng.wait_ge(S("g_act"), c + 1)
                    else:
                        eng.wait_ge(S("u_mul"), 3 * t + c - 5)
                    if c == 0:
                        eng.wait_ge(S("xt_lo"), t + 1)
                ins = project(p, wg_hi, wg_lo, c, k)
                if k == KB - 1:
                    ins.then_inc(S("g_mm"), 1)

            def gate(t, p):
                for c in range(NC_):
                    for k in range(KB):
                        gate_block(t, p, c, k)

            def up_block(t, p, c, k):
                if k == 0:
                    if isinstance(t, int) and t == 0:
                        eng.wait_ge(S("w_lo"), N_WG + GRP[c][-1] + 1)
                    if isinstance(t, int) and t == NT - 1:
                        eng.wait_ge(S("u_mul"), 3 * t - 3 + c + 1)
                    else:
                        eng.wait_ge(S("g_act"), 3 * t + 3 + c + 1)
                ins = project(p, wu_hi, wu_lo, c, k)
                if k == KB - 1:
                    ins.then_inc(S("u_mm"), 1)

            def up(t, p, c):
                for k in range(KB):
                    up_block(t, p, c, k)

            def count_good(t, bk):
                eng.wait_ge(S("sel_done"), done("sel_done", t + 1))
                eng.matmul(bk[0:1, 0:1], good, one_c, start=True, stop=True).then_inc(S("flag_mm"), 1)

            def h_transpose(t, g):
                eng.wait_ge(S("h_done"), 3 * t + g + 1)
                eng.wait_ge(S("ht_lo"), 3 * t + g + 1)
                for k, b in enumerate(GRP[g]):
                    ins = eng.transpose(tp[g][0:IW[b], P * k:P * k + P], h_buf[:, P * b:P * b + IW[b]],
                                        ident[:, :])
                ins.then_inc(S("ht_tr"), 1)

            def down(t, g, b_):
                eng.wait_ge(S("ht_lo"), done("ht_lo", 3 * t + g + 1))
                if g == 0:
                    eng.wait_ge(S("y_done"), t + 1)
                for k, b in enumerate(GRP[g]):
                    w = IW[b]
                    hi, lo = ht_hi[b_][0:w, k, :], ht_lo[b_][0:w, k, :]
                    eng.matmul(dn[:, :], hi, wd_hi[0:w, b, :], start=(b == 0), stop=False)
                    eng.matmul(dn[:, :], hi, wd_lo[0:w, b, :], start=False, stop=False)
                    ins = eng.matmul(dn[:, :], lo, wd_hi[0:w, b, :], start=False, stop=(b == IB - 1))
                ins.then_inc(S("d_mm"), 1)

            eng.wait_ge(S("consts"), 1)
            for e in prologue():
                if e[0] == "w":
                    weights_transpose(e[1])
                elif e[0] == "x":
                    x_transpose(e[1], e[1])
                else:
                    _, kind, t, c, k = e
                    (gate_block if kind == "g" else up_block)(t, t, c, k)
            eng.wait_ge(S("w_lo"), N_ALL)
            count_good(0, xb)
            h_transpose(0, 0)

            def turn(t, p, more=True):
                q = 1 - p
                if more:
                    x_transpose(t + 2, p)
                h_transpose(t, 1)
                down(t, 0, p)
                h_transpose(t, 2)
                down(t, 1, q)
                down(t, 2, p)
                if more:
                    gate(t + 2, p)
                    up(t + 1, q, 0)
                    count_good(t + 1, xb)
                    up(t + 1, q, 1)
                    h_transpose(t + 1, 0)
                    up(t + 1, q, 2)

            turns(eng, turn)
            turn(NT - 2, 0, more=False)

            def x2t_transpose(t):
                eng.wait_ge(S("x16"), t + 1)
                if t < 2:
                    eng.wait_ge(S("ht_lo"), done("ht_lo", 3 * (NT - 2) + 2 + t))
                if t >= 2:
                    eng.wait_ge(S("x2t_ev"), t - 1)
                bk = x2t_bank(t)[:, :].bitcast(f16)
                for j in range(2 * KB):
                    ins = eng.transpose(bk[:, P * j:P * j + P],
                                        x16[:, t * 2 * HD + P * j:t * 2 * HD + P * j + P], ident16[:, :])
                ins.then_inc(S("x2t_tr"), 1)

            def vgu_transpose(m):
                if not (isinstance(m, int) and m == 0):
                    eng.wait_ge(S("vgu_ev"), m)
                bk = t2gu[:, :].bitcast(f16)
                for w, src in enumerate((ng, nu)):
                    for k in range(KB):
                        o = (w * KB + k) * P
                        ins = eng.transpose(bk[:, o:o + P],
                                            src[:, bass.ds(m, 1), P * k:P * k + P].rearrange("p a c -> p (a c)"),
                                            ident16[:, :])
                ins.then_inc(S("vgu_tr"), 1)

            def vd_transpose(m):
                if not (isinstance(m, int) and m == 0):
                    eng.wait_ge(S("vd_ev"), m)
                bk = t2d[:, :].bitcast(f16)
                for hb in range(KB):
                    ins = eng.transpose(bk[:, P * hb:P * hb + P], nd[:, hb, bass.ds(m * P, P)], ident16[:, :])
                ins.then_inc(S("vd_tr"), 1)

            def gate_up2(q, m, half):
                tok = slice(half * HALF, half * HALF + HALF)
                for w, bk in enumerate((g2, u2)):
                    if not (isinstance(q, int) and q == 0):
                        eng.wait_ge(S(("sg_done", "h2_done")[w]), q)
                    for k in range(KB):
                        for part in range(2):
                            ins = eng.matmul(bk[:, :], vgu[:, w * KB + k, bass.ds(m * P, P)],
                                             x2t[part][:, k, tok], start=(k + part == 0),
                                             stop=(k == KB - 1 and part == 1))
                    ins.then_inc(S(("g2_mm", "u2_mm")[w]), 1)

            def down2(q, m, p, j, first, last):
                if first and q:
                    eng.wait_ge(S("y2_done"), j + 1)
                c = slice(P * j, P * j + P)
                rhs = vd[:, bass.ds(m, 1), :].rearrange("p a c -> p (a c)")
                eng.matmul(acc[j][:, :], h2_hi[p][:, c], rhs, start=first, stop=False)
                eng.matmul(acc[j][:, :], h2_lo[p][:, c], rhs, start=False, stop=last
                           ).then_inc(S("dn_mm"), 1)

            T = NT - 1
            for c in range(NC_):
                up(T, 1, c)
                x2t_transpose(c)
            eng.wait_ge(S("n2_0"), 32)
            vgu_transpose(0)
            x2t_transpose(TH - 1)
            count_good(T, tp[0])
            eng.wait_ge(S("vgu_ev"), 1)
            eng.wait_ge(S("x2t_ev"), TH)
            eng.wait_ge(S("u_mul"), 3 * NT)
            gate_up2(0, 0, 0)
            vgu_transpose(1)
            eng.wait_ge(S("flag_read"), NT)
            h_transpose(T, 0)
            h_transpose(T, 1)
            down(T, 0, 1)
            h_transpose(T, 2)
            down(T, 1, 0)
            down(T, 2, 1)
            eng.wait_ge(S("n2_1"), 32)
            eng.wait_ge(S("nd"), 16)

            def step2(q, p, half):
                m = q - half * MB
                at_ = q if isinstance(q, int) else None
                if half == 0 and not (at_ is not None and at_ >= MB - 2):
                    if at_ == 1:
                        eng.wait_ge(S("x2t_ev"), TH + 1)
                    vgu_transpose(q + 2)
                if half == 0:
                    vd_transpose(q)
                if at_ == MB - 2:
                    eng.wait_ge(S("vgu_ev"), MB)
                    x2t_transpose(X2T_AT[at_][0])
                if at_ == MB - 1:
                    eng.wait_ge(S("x2t_ev"), NT)
                    gate_up2(q + 1, 0, 1)
                elif at_ != 2 * MB - 1:
                    if half == 0:
                        eng.wait_ge(S("vgu_ev"), q + 2)
                    gate_up2(q + 1, m + 1, half)
                if at_ in X2T_AT:
                    t = X2T_AT[at_][-1]
                    if t < NT - 1:
                        eng.wait_ge(S("vgu_ev"), at_ + 3)
                    else:
                        eng.wait_ge(S("x2t_ev"), NT - 1)
                    x2t_transpose(t)
                if half == 0:
                    eng.wait_ge(S("vd_ev"), q + 1)
                if at_ is not None and at_ >= LAST:
                    if at_ == 2 * MB - 1:
                        order = [(b, j) for b in range(LAST, at_) for j in range(2)]
                        order += [(at_, 0), (at_, 1)]
                        order += [(b, j) for j in range(2, TH) for b in range(LAST, at_ + 1)]
                        for b, j in order:
                            eng.wait_ge(S("h2_lo"), b + 1)
                            down2(b, b - MB, b - LAST, j, False, b == at_)
                    return
                eng.wait_ge(S("h2_lo"), q + 1)
                for j in range(TH):
                    if at_ == 0 and j == TH - 1:
                        eng.wait_ge(S("y_done"), done("y_done", NT))
                    down2(q, m, p, j, at_ in (0, MB), at_ == MB - 1)
                if at_ == 1:
                    eng.wait_ge(S("n2_2"), 32)
                    eng.wait_ge(S("x2t_ev"), TH + 2)

            steps2(eng, step2)


_INS = ['L0_attn_x', 'L0_attn_w_gate', 'L0_attn_w_up', 'L0_attn_w_down',
        'L0_ffn_W_gate', 'L0_ffn_W_up', 'L0_ffn_W_down']
_OUTS = [((4, 256, 512), 'float32')]


def kernel(**inputs):
    import numpy as _np
    import concourse.bacc as _bacc
    from concourse import mybir as _mybir
    from concourse.bass_utils import run_bass_kernel_spmd as _run

    nc = _bacc.Bacc("TRN2", target_bir_lowering=False, num_devices=1)
    arrays, args = {}, []
    for name in _INS:
        a = _np.ascontiguousarray(inputs[name])
        arrays[f"in_{name}_dram"] = a
        args.append(nc.dram_tensor(f"in_{name}_dram", a.shape, _mybir.dt.from_np(a.dtype), kind="ExternalInput").ap())
    for i, (shape, dtype) in enumerate(_OUTS):
        dt = _mybir.dt.from_np(_np.dtype(dtype))
        args.append(nc.dram_tensor(f"out_{i}_dram", shape, dt, kind="ExternalOutput").ap())
    build(nc, *args)
    r = _run(nc, [arrays], core_ids=[0])
    return r.results[0]["out_0_dram"]
```

```python
import concourse.bass as bass
from concourse import mybir
from contextlib import ExitStack


def build(nc, x, w_gate, w_up, w_down, v_gate, v_up, v_down, out):
    f32, f32r = mybir.dt.float32, mybir.dt.float32r
    f16, i32, i8 = mybir.dt.float16, mybir.dt.int32, mybir.dt.int8
    ALU, ACT = mybir.AluOpType, mybir.ActivationFunctionType

    P = 128
    HD = x.shape[2]
    TOK = x.shape[0] * x.shape[1]
    NT = TOK // P
    KB = HD // P
    I = w_gate.shape[1]
    IB = -(-I // P)
    IW = [min(P, I - P * b) for b in range(IB)]
    CH = [(c, min(c + 512, I)) for c in range(0, I, 512)]
    NC_ = len(CH)
    GRP = [list(range(4 * g, min(4 * g + 4, IB))) for g in range(NC_)]
    ZERO = I // 2
    M2 = v_gate.shape[1]
    MB = M2 // P
    HALF = TOK // 2
    TH = HALF // P
    KEEP = 6
    LAST = 2 * MB - KEEP
    UP = 1024.0
    EPS = 1e-5
    START, SLOPE, AIM, NEAR = 0.782, 655.0, ZERO + 8, 7.5
    PASSES = 4
    WARM = 8

    xf = x.rearrange("b s h -> (b s) h")
    of = out.rearrange("b s h -> (b s) h")
    x2_dram = nc.dram_tensor("x2_scratch", [TOK, HD], f32).ap()

    ctx = ExitStack()
    with ctx:
        base = -(-nc.sbuf_base // 64) * 64
        at = [base]

        def place(name, shape, dt, size, offset=None):
            if offset is None:
                offset = at[0]
                at[0] += -(-size // 32) * 32
            return nc.alloc_sbuf_tensor_at(name, [P] + shape, dt, offset=offset), offset

        wg_hi, A0 = place("wg_hi", [KB, I], f32r, KB * I * 4)
        wg_lo, _ = place("wg_lo", [KB, I], f32r, KB * I * 4)
        wu_hi, B0 = place("wu_hi", [KB, I], f32r, KB * I * 4)
        wu_lo, _ = place("wu_lo", [KB, I], f32r, KB * I * 4)
        wd_hi, C0 = place("wd_hi", [IB, HD], f32r, IB * HD * 4)
        wd_lo, _ = place("wd_lo", [IB, HD], f32r, IB * HD * 4)
        w_raw = [place("wg_raw", [KB, I], f32, 0, A0 + KB * I * 4)[0],
                 place("wu_raw", [KB, I], f32, 0, B0 + KB * I * 4)[0],
                 place("wd_raw", [IB, HD], f32, 0, C0 + IB * HD * 4)[0]]
        x16, X0 = place("x16", [NT * 2 * HD], f16, NT * 2 * HD * 2)
        x_in0, XI0 = place("x_in0", [HD], f32, HD * 4)
        x_in1, _ = place("x_in1", [HD], f32, HD * 4)
        x_in = [x_in0, x_in1]
        x_res, _ = place("x_res", [HD], f32, HD * 4)
        x2, _ = place("x2", [HD], f32, HD * 4)
        xt_hi0, XT0 = place("xt_hi0", [KB, P], f32r, HD * 4)
        xt_lo0, _ = place("xt_lo0", [KB, P], f32r, HD * 4)
        xt_hi1, _ = place("xt_hi1", [KB, P], f32r, HD * 4)
        xt_lo1, _ = place("xt_lo1", [KB, P], f32r, HD * 4)
        xt_hi, xt_lo = [xt_hi0, xt_hi1], [xt_lo0, xt_lo1]
        s0, S0 = place("s0", [I], f32, I * 4)
        a0, _ = place("a0", [I], f32, I * 4)
        s1, _ = place("s1", [I], f32, I * 4)
        a1, _ = place("a1", [I], f32, I * 4)
        s_buf, a_buf = [s0, s1], [a0, a1]
        h_buf, _ = place("h_buf", [I], f32, I * 4)
        ht_hi = [place(f"ht_hi{i}", [4, P], f32r, 2048)[0] for i in range(2)]
        ht_lo = [place(f"ht_lo{i}", [4, P], f32r, 2048)[0] for i in range(2)]
        signs, _ = place("signs", [I], i8, I)
        ident, _ = place("ident", [P], f32, P * 4)
        ident16, _ = place("ident16", [P], f16, P * 2)
        rank, _ = place("rank", [17], f32, 17 * 4)
        top, _ = place("top", [16], f32, 64)
        small, _ = place("small", [64], f32, 256)
        ints, _ = place("ints", [8], i32, 32)
        x2t_hi, _ = place("x2t_hi", [KB, TOK], f16, KB * TOK * 2)
        assert at[0] <= nc.sbuf_usable_end, (at[0], nc.sbuf_usable_end)
        vgu, _ = place("vgu", [2 * KB, M2], f16, 0, A0)
        vd16, _ = place("vd16", [MB, HD], f16, 0, A0 + 2 * KB * M2 * 2)
        assert A0 + 3 * KB * M2 * 2 <= B0
        vd, _ = place("vd", [MB, HD], f32r, 0, B0)
        R0 = B0 + MB * HD * 4
        res = [place(f"res{j}", [HD], f32, 0, R0 + j * HD * 4)[0] for j in range(TH)]
        slots = [R0 + TH * HD * 4] + [C0 + i * 4096 for i in range(KEEP - 1)]
        assert slots[0] + 4096 <= C0 and slots[-1] + 4096 <= X0
        h2_hi = [place(f"h2_hi{i}", [HALF], f32r, 0, o)[0] for i, o in enumerate(slots)]
        h2_lo = [place(f"h2_lo{i}", [HALF], f32r, 0, o + 2048)[0] for i, o in enumerate(slots)]
        sg = [place(f"sg{i}", [HALF], f32, 0, XI0 + i * 2048)[0] for i in range(2)]
        h2 = [place(f"h2{i}", [HALF], f32, 0, XT0 + i * 2048)[0] for i in range(2)]
        x2t = [x2t_hi, place("x2t_lo", [KB, TOK], f16, 0, S0)[0]]

        cols = iter(range(64))

        def col(n=1):
            c = [next(cols) for _ in range(n)]
            return small[:, c[0]:c[-1] + 1]

        half_c, one_c, good, keep, below, cnt, jj, jok = (col() for _ in range(8))
        abs_sum, sign_sum, err, far, step, neg_t, unit, unit2 = (col() for _ in range(8))
        start_c, unit_c, unit2_c, aim_c, minus_c, warm = (col() for _ in range(6))
        pos_t = [col(), col()]
        stats, mv, rstd, var_e = col(6), col(2), col(), col()
        stats2, mv2, rstd2, var_e2 = col(6), [col(2) for _ in range(TH)], col(TH), col(TH)
        tie_m, le = col(), col()
        bit, found, tried, gain, n_good = (ints[:, i:i + 1] for i in range(5))

        def bank(name):
            return ctx.enter_context(nc.psum_tensor(name, [P, 512], f32))

        gu = [bank(f"gu{i}") for i in range(3)]
        tp = [bank(f"tp{i}") for i in range(3)]
        dn = bank("dn")
        xb = bank("xb")
        g2, u2 = [gu[0], gu[2]], [gu[1], xb]
        acc = [tp[0], tp[1], tp[2], dn]

        def up_bank(t, c):
            return tp[c] if isinstance(t, int) and t == 1 else gu[c]

        def x2t_bank(t):
            return tp[1 + t % 2] if t < NT - 2 else gu[t - NT + 2]

        def good_bank(t):
            return dn if is_first(t) else tp[0] if isinstance(t, int) and t == NT - 1 else xb

        sem = {}

        def S(name):
            if name not in sem:
                sem[name] = ctx.enter_context(nc.semaphore(name))
            return sem[name]

        CR = {"sel_done": 1, "y_done": 1, "ht_lo": 3, "d_mm": 2, "x2_saved": 16}

        def done(name, n):
            return n + CR.get(name, 0)

        TURNS = NT - 2

        def turns(eng, body):
            with eng.Fori(2, TURNS - 1, 2) as i:
                body(i, 0)
                body(i + 1, 1)

        def is_first(t):
            return isinstance(t, int) and t == 0

        PIECES = [(w, c, k) for w in range(2) for c in range(NC_) for k in range(KB)]
        N_WU = len(PIECES) // 2
        PIECES += [(2, 0, b) for b in range(IB)]
        N_W = len(PIECES)
        N_LIST = N_W - 5

        def piece(n):
            w, c, k = PIECES[n]
            hi, lo = ((wg_hi, wg_lo), (wu_hi, wu_lo), (wd_hi, wd_lo))[w]
            if w < 2:
                at_ = (slice(0, P), k, slice(*CH[c]))
            else:
                at_ = (slice(0, IW[k]), k, slice(0, HD))
            return w_raw[w][at_], hi[at_], lo[at_]

        LOADS = [1] * KB + [2] * 10 + [4, 4, 2, 1]
        assert sum(LOADS) == N_W
        load_of = [n for n, c in enumerate(LOADS) for _ in range(c)]

        def prologue():
            n = 4
            yield ("x", 0)
            for k in range(n):
                yield ("w", k)
            for kind, t in (("g", 0), ("g", 1), ("u", 0)):
                for c in range(NC_):
                    if kind == "g" and t == 0 and c == 1:
                        yield ("x", 1)
                    if kind == "u" and c == NC_ - 1:
                        yield ("x", 2)
                    for k in range(KB):
                        yield ("mm", kind, t, c, k)
                        if n < N_LIST:
                            yield ("w", n)
                            n += 1
            assert n == N_LIST

        def steps2(eng, fn):
            for q in range(2):
                fn(q, q % 2, 0)
            with eng.Fori(2, MB - 3, 2) as i:
                fn(i, 0, 0)
                fn(i + 1, 1, 0)
            fn(MB - 2, 0, 0)
            fn(MB - 1, 1, 0)
            for q in range(2):
                fn(MB + q, q, 1)
            with eng.Fori(MB + 2, LAST - 1, 2) as i:
                fn(i, 0, 1)
                fn(i + 1, 1, 1)
            for q in range(LAST, 2 * MB):
                fn(q, q % 2, 1)

        def slot(q, p):
            return q - LAST if isinstance(q, int) and q >= LAST else p

        block = ctx.enter_context(nc.Block())

        @block.sync
        def _(eng):
            eng.nop().then_inc(S("x2_saved"), 16)
            n = 0
            for i, c in enumerate(LOADS):
                w, chunk, k = PIECES[n]
                if w < 2:
                    lo, hi = CH[chunk]
                    src = (w_gate, w_up)[w][P * k:P * (k + c), lo:hi].rearrange("(k p) c -> p k c", p=P)
                    dst = w_raw[w][:, k:k + c, lo:hi]
                elif IW[k] == P:
                    src = w_down[P * k:P * (k + c), :].rearrange("(k p) c -> p k c", p=P)
                    dst = w_raw[w][:, k:k + c, :]
                else:
                    src = w_down[P * k:I, :]
                    dst = w_raw[w][0:IW[k], k, :]
                eng.dma_start(dst, src).then_inc(S(f"w_load{i}"), 16)
                n += c

            def load_next(t, p):
                eng.wait_ge(S("x_tr"), t + 1)
                eng.dma_start(x_in[p][:, :], xf[bass.ds(t * P + 2 * P, P), :]).then_inc(S(f"x_loaded{p}"), 16)

            def load_residual(t):
                eng.wait_ge(S("y_done"), t + 1)
                eng.dma_start(x_res[:, :], xf[bass.ds(t * P, P), :]).then_inc(S("xr_loaded"), 16)

            def save_x2(t):
                eng.wait_ge(S("x2_done"), t + 1)
                eng.dma_start(x2_dram[bass.ds(t * P, P), :], x2[:, :]).then_inc(S("x2_saved"), 16)

            def turn(t, p, more=True):
                load_residual(t)
                if more:
                    load_next(t + 1, 1 - p)
                save_x2(t)

            load_next(0, 0)
            with eng.Fori(0, TURNS - 3, 2) as i:
                turn(i, 0)
                turn(i + 1, 1)
            turn(TURNS - 2, 0)
            load_residual(TURNS - 1)

            eng.wait_ge(S("g_mm"), 3 * NT)
            for w, src in enumerate((v_gate, v_up)):
                eng.dma_start(vgu[:, w * KB:w * KB + KB, :], src.rearrange("(k p) m -> p k m", p=P)
                              ).then_inc(S("vgu"), 16)
            eng.dma_start(vd16[:, :, :], v_down.rearrange("(m p) h -> p m h", p=P)).then_inc(S("vd16"), 16)
            load_residual(NT - 2)
            save_x2(NT - 3)
            load_residual(NT - 1)
            save_x2(NT - 2)
            save_x2(NT - 1)
            eng.wait_ge(S("x2_saved"), 16 * (NT + 1))
            for j in range(TH):
                eng.dma_start(res[j][:, :], x2_dram[P * j:P * j + P, :]).then_inc(S("res"), 16)
            for half in range(2):
                for j in range(TH):
                    t = TH * half + j
                    eng.wait_ge(S("o_done"), t + 1)
                    eng.dma_start(of[P * t:P * t + P, :], res[j][:, :]).then_inc(S("out"), 16)
                if half == 0:
                    eng.wait_ge(S("out"), 16 * TH)
                    for j in range(TH):
                        t = TH + j
                        eng.dma_start(res[j][:, :], x2_dram[P * t:P * t + P, :]).then_inc(S("res"), 16)
            eng.wait_ge(S("out"), 16 * NT)

        @block.gpsimd
        def _(eng):
            def unit_matrix(m):
                eng.memset(m[:, :], 0.0)
                eng.drain()
                return eng.affine_select(out=m[:, :], in_=m[:, :], compare_op=ALU.not_equal, fill=1.0,
                                         base=0, pattern=[[-1, P]], channel_multiplier=1)

            unit_matrix(ident).then_inc(S("ident"), 1)
            unit_matrix(ident16)
            eng.memset(half_c, -0.5)
            eng.memset(one_c, 1.0)
            eng.memset(minus_c, -1.0)
            eng.memset(start_c, -START / I)
            eng.memset(unit_c, -0.5 * START / I / SLOPE)
            eng.memset(unit2_c, -0.5 * 0.85 * START / I / SLOPE)
            eng.memset(aim_c, float(I - 2 * AIM))
            for k in range(17):
                eng.memset(rank[:, k:k + 1], float(k - 1))
            eng.drain()
            eng.nop().then_inc(S("consts"), 1)

            def search_start(t):
                eng.wait_ge(S("abs_done"), t + 1)
                eng.tensor_tensor(unit, abs_sum, unit_c, ALU.mult)
                eng.tensor_tensor(unit2, abs_sum, unit2_c, ALU.mult)
                eng.tensor_tensor(neg_t, abs_sum, start_c, ALU.mult).then_inc(S("thr"), 1)
                eng.drain()

            def rstd_of(t):
                eng.wait_ge(S("var_done"), t + 1)
                eng.tensor_tensor(rstd, var_e, half_c, ALU.pow).then_inc(S("rstd"), 1)

            wd_pieces = iter(range(2 * N_WU, N_W))

            def wd_low():
                n = next(wd_pieces, None)
                if n is not None:
                    raw, hi, lo = piece(n)
                    eng.wait_ge(S("w_hi"), n + 1)
                    eng.tensor_tensor(lo, raw, hi, ALU.subtract).then_inc(S("wd_lo"), 1)

            def search_moves(t, passes, p, reused):
                for n in passes:
                    eng.wait_ge(S("counted"), t * PASSES + n + 1)
                    eng.tensor_tensor(err, sign_sum, aim_c, ALU.subtract)
                    eng.drain()
                    eng.tensor_scalar(far, err, err, 4 * NEAR * NEAR, ALU.mult, ALU.is_gt)
                    eng.tensor_scalar(step, err, unit if n < 2 else unit2, None, ALU.mult)
                    eng.drain()
                    last = n == PASSES - 1
                    ins = eng.tensor_scalar(neg_t, step, far, neg_t, ALU.mult, ALU.add)
                    if last:
                        eng.drain()
                        if reused:
                            eng.wait_ge(S("sel_done"), t)
                        ins = eng.tensor_tensor(pos_t[p], neg_t, minus_c, ALU.mult)
                    ins.then_inc(S("thr"), 1)
                    eng.drain()
                    if isinstance(t, int) and t == 1:
                        wd_low()
                        wd_low()

            search_start(0)
            search_moves(0, range(PASSES), 0, False)
            search_start(1)
            wd_low()
            search_moves(1, range(2), 1, False)

            def turn(t, p, more=True):
                search_moves(t + 1, range(2, PASSES), 1 - p, True)
                if is_first(t):
                    for n in range(IB):
                        wd_low()
                if more:
                    search_start(t + 2)
                    search_moves(t + 2, range(2), p, True)
                rstd_of(t)

            turn(0, 0)
            turn(1, 1)
            turns(eng, turn)
            turn(NT - 2, 0, more=False)
            rstd_of(NT - 1)
            for t in range(NT):
                eng.wait_ge(S("var2_done"), t + 1)
                j = t % TH
                eng.tensor_tensor(rstd2[:, j:j + 1], var_e2[:, j:j + 1], half_c, ALU.pow).then_inc(S("rstd2"), 1)

        @block.scalar
        def _(eng):
            def x_hi(t, p):
                eng.wait_ge(S("x_tr"), t + 1)
                eng.activation(xt_hi[p][:, :, :], xb[:, :].rearrange("p (k c) -> p k c", k=KB),
                               ACT.Copy).then_inc(S("xt_hi"), 1)

            def weights_hi(n):
                raw, hi, _ = piece(n)
                eng.wait_ge(S(f"w_load{load_of[n]}"), 16)
                eng.activation(hi, raw, ACT.Copy).then_inc(S("w_hi"), 1)

            def silu(t, p, c):
                lo, hi = CH[c]
                eng.wait_ge(S("g_mm"), 3 * t + c + 1)
                eng.activation(s_buf[p][:, lo:hi], gu[c][:, 0:hi - lo], ACT.Silu).then_inc(S("g_act"), 1)

            def absolute(t, p):
                eng.wait_ge(S("g_act"), 3 * t + 3)
                eng.activation(a_buf[p][:, :], s_buf[p][:, :], ACT.Abs,
                               accum_out=abs_sum).then_inc(S("abs_done"), 1)

            def count(t, p, n):
                eng.wait_ge(S("thr"), t * (PASSES + 1) + n + 1)
                eng.wait_ge(S("abs_done"), t + 1)
                eng.activation(signs[:, :], a_buf[p][:, :], ACT.Sign, bias=neg_t,
                               accum_out=sign_sum).then_inc(S("counted"), 1)

            def h_hi(t, g, b):
                eng.wait_ge(S("ht_tr"), 3 * t + g + 1)
                eng.wait_ge(S("d_mm"), 3 * t + g + 1)
                w = P * len(GRP[g])
                eng.activation(ht_hi[b][:, 0:len(GRP[g]), :],
                               tp[g][:, 0:w].rearrange("p (k c) -> p k c", c=P),
                               ACT.Copy).then_inc(S("ht_hi"), 1)

            for t in range(2):
                eng.dma_start(x_in[t][:, :], xf[P * t:P * t + P, :]).then_inc(S(f"x_loaded{t}"), 16)
            eng.wait_ge(S("consts"), 1)
            eng.activation(warm, one_c, ACT.Silu)
            counts = {("g", 1, 0): (0, 0), ("g", 1, 4): (0, 1), ("g", 1, 8): (0, 2)}
            for e in prologue():
                if e[0] == "w":
                    weights_hi(e[1])
                elif e[0] == "x":
                    if e[1] < 2:
                        x_hi(e[1], e[1])
                else:
                    _, kind, t, c, k = e
                    if kind == "g" and k == KB - 1:
                        silu(t, t, c)
                        if (t, c) == (1, NC_ - 1):
                            count(0, 0, 3)
                        if c == NC_ - 1:
                            absolute(t, t)
                    if (kind, t, KB * c + k) in counts:
                        tile, n = counts[kind, t, KB * c + k]
                        count(tile, tile, n)

            def x_hi_next(t, p):
                eng.wait_ge(S("u_mm"), 3 * t + 3)
                x_hi(t + 2, p)

            def silus(t, p, chunks=range(NC_)):
                if 0 in chunks:
                    eng.wait_ge(S("h_done"), 3 * t - 3)
                for c in chunks:
                    silu(t, p, c)

            x_hi_next(0, 0)
            for n in range(PASSES):
                count(1, 1, n)
                for k in range(N_LIST + 2 * n, min(N_LIST + 2 * n + 2, N_W)):
                    weights_hi(k)
            x_hi_next(1, 1)
            h_hi(0, 0, 0)
            h_hi(0, 1, 1)
            silus(2, 0, (0, 1))
            h_hi(0, 2, 0)
            silus(2, 0, (2,))
            absolute(2, 0)
            count(2, 0, 0)
            count(2, 0, 1)
            count(2, 0, 2)
            count(2, 0, 3)
            h_hi(1, 0, 1)
            h_hi(1, 1, 0)
            silus(3, 1, (0, 1))
            h_hi(1, 2, 1)
            silus(3, 1, (2,))
            absolute(3, 1)
            count(3, 1, 0)
            h_hi(2, 0, 0)
            count(3, 1, 1)

            def turn(t, p, more=True):
                q = 1 - p
                if more:
                    x_hi_next(t, p)
                h_hi(t, 1, q)
                count(t + 1, q, 2)
                h_hi(t, 2, p)
                count(t + 1, q, 3)
                if more:
                    silus(t + 2, p)
                    absolute(t + 2, p)
                    count(t + 2, p, 0)
                    h_hi(t + 1, 0, q)
                    count(t + 2, p, 1)

            turns(eng, turn)
            turn(NT - 2, 0, more=False)

            def x2t_copy(t):
                eng.wait_ge(S("x2t_tr"), t + 1)
                src = x2t_bank(t)[:, :].bitcast(f16).rearrange("p (a k c) -> p a k c", a=2, c=P)
                for part in range(2):
                    ins = eng.activation(x2t[part][:, :, P * t:P * t + P], src[:, part], ACT.Copy)
                ins.then_inc(S("x2t_ev"), 1)

            def vd_copy(m):
                eng.activation(vd[:, bass.ds(m, 1), :], vd16[:, bass.ds(m, 1), :], ACT.Copy
                               ).then_inc(S("vd_ev"), 1)

            def gate2(q, p):
                eng.wait_ge(S("g2_mm"), q + 1)
                if not (isinstance(q, int) and q < 2):
                    eng.wait_ge(S("h2_done"), q - 1)
                eng.activation(sg[p][:, :], g2[p][:, :], ACT.Silu, scale=1.0 / UP).then_inc(S("sg_done"), 1)

            def h2_high(q, p):
                eng.wait_ge(S("h2_done"), q + 1)
                if not (isinstance(q, int) and (q < 2 or q >= LAST + 2)):
                    eng.wait_ge(S("dn_mm"), 4 * q - 4)
                eng.activation(h2_hi[slot(q, p)][:, :], h2[p][:, :], ACT.Copy).then_inc(S("h2_hi"), 1)

            eng.wait_ge(S("h_done"), 3 * (NT - 1))
            for t in range(NT - 2):
                x2t_copy(t)
            eng.wait_ge(S("u_mm"), 3 * NT)
            eng.wait_ge(S("vd16"), 16)
            vd_copy(0)
            vd_copy(1)
            gate2(0, 0)
            gate2(1, 1)
            h_hi(NT - 1, 0, (NT - 1) % 2)
            h_hi(NT - 1, 1, NT % 2)
            h2_high(0, 0)
            h_hi(NT - 1, 2, (NT - 1) % 2)
            eng.wait_ge(S("d_mm"), done("d_mm", 3 * NT))

            def step2(q, p, half):
                at_ = q if isinstance(q, int) else None
                if at_ not in (0, 1):
                    gate2(q, p)
                if at_ == MB - 2:
                    x2t_copy(NT - 2)
                if at_ != 0:
                    h2_high(q, p)
                if half == 0 and not (at_ is not None and at_ >= MB - 2):
                    vd_copy(q + 2)
                if at_ == MB - 2:
                    x2t_copy(NT - 1)

            steps2(eng, step2)

        @block.vector
        def _(eng):
            v = nc.vector
            for name, n in CR.items():
                if name in ("sel_done", "y_done", "ht_lo"):
                    eng.nop().then_inc(S(name), n)

            v.memset(tp[2][:, P * len(GRP[2]) - P:P * len(GRP[2])], 0.0)

            def x_low(t, p):
                eng.wait_ge(S("xt_hi"), t + 1)
                v.tensor_tensor(xt_lo[p][:, :, :], xb[:, :].rearrange("p (k c) -> p k c", k=KB),
                                xt_hi[p][:, :, :], ALU.subtract).then_inc(S("xt_lo"), 1)

            def weights_lo(n):
                raw, hi, lo = piece(n)
                eng.wait_ge(S("w_hi"), n + 1)
                v.tensor_tensor(lo, raw, hi, ALU.subtract).then_inc(S("w_lo"), 1)

            def select(t, p, part=None):
                a = a_buf[p]
                if part in (None, 0):
                    eng.wait_ge(S("thr"), t * (PASSES + 1) + PASSES + 1)
                    eng.wait_ge(S("abs_done"), t + 1)
                    v.tensor_scalar(h_buf[:, :], a[:, :], pos_t[p], None, ALU.is_lt, ALU.add, accum_out=cnt)
                    eng.drain()
                if part in (None, 1):
                    v.scalar_tensor_tensor(h_buf[:, :], a[:, :], pos_t[p], a[:, :], ALU.is_lt, ALU.mult)
                    eng.drain()
                if part in (None, 2):
                    v.tensor_scalar(jj, cnt, float(ZERO + 1), None, ALU.subtract)
                    v.max(top[:, 0:8], h_buf[:, :])
                    eng.drain()
                if part in (None, 3):
                    v.tensor_scalar(jok, jj, 14.5, None, ALU.is_le)
                    v.match_replace(h_buf[:, :], top[:, 0:8], h_buf[:, :], -1.0)
                    eng.drain()
                if part in (None, 4):
                    v.max(top[:, 8:16], h_buf[:, :])
                    eng.drain()
                    v.scalar_tensor_tensor(h_buf[:, 0:16], rank[:, 1:17], jj, top[:, :], ALU.is_equal,
                                           ALU.mult, accum_out=keep)
                    v.scalar_tensor_tensor(h_buf[:, 16:32], rank[:, 0:16], jj, top[:, :], ALU.is_equal,
                                           ALU.mult, accum_out=below)
                    eng.drain()
                    v.tensor_scalar(good, keep, below, jok, ALU.is_gt, ALU.mult).then_inc(S("sel_done"), 1)

            def up_times_s(t, p, c):
                lo, hi = CH[c]
                eng.wait_ge(S("u_mm"), 3 * t + c + 1)
                eng.wait_ge(S("abs_done"), t + 1)
                v.tensor_tensor(s_buf[p][:, lo:hi], up_bank(t, c)[:, 0:hi - lo], s_buf[p][:, lo:hi],
                                ALU.mult).then_inc(S("u_mul"), 1)

            def settle(t, p):
                a, found_f = a_buf[p], found.bitcast(f32)
                eng.wait_ge(S("flag_mm"), t + 1)
                bk = good_bank(t)
                v.tensor_copy(n_good[0:1, :], bk[0:1, 0:1]).then_inc(S("flag_read"), 1)
                eng.drain()
                n = eng.value_load(n_good[0:1, :], min_val=0, max_val=P)
                with eng.If(n != P):
                    v.memset(bit.bitcast(f32), 2.0)
                    v.memset(found, 0)
                    eng.drain()
                    with eng.Fori(0, 31):
                        v.tensor_tensor(tried, found, bit, ALU.bitwise_or)
                        eng.drain()
                        v.tensor_scalar(h_buf[:, :], a[:, :], tried.bitcast(f32), None, ALU.is_lt,
                                        ALU.add, accum_out=cnt)
                        eng.drain()
                        v.tensor_scalar(le, cnt, ZERO - 0.5, None, ALU.is_le)
                        eng.drain()
                        v.tensor_scalar(gain, bit, le, None, ALU.mult)
                        eng.drain()
                        v.tensor_tensor(found, found, gain, ALU.bitwise_or)
                        v.tensor_scalar(bit, bit, 1, None, ALU.logical_shift_right)
                        eng.drain()
                    v.tensor_scalar(h_buf[:, :], a[:, :], found_f, None, ALU.is_lt, ALU.add, accum_out=cnt)
                    eng.drain()
                    v.tensor_scalar(tie_m, cnt, -1.0, float(ZERO), ALU.mult, ALU.add)
                    v.tensor_scalar(h_buf[:, :], a[:, :], found_f, None, ALU.is_equal)
                    eng.drain()
                    v.tensor_tensor_scan(h_buf[:, :], h_buf[:, :], h_buf[:, :], 0.0, ALU.add, ALU.max)
                    eng.drain()
                    v.tensor_scalar(h_buf[:, :], h_buf[:, :], tie_m, None, ALU.is_le)
                    eng.drain()
                    v.scalar_tensor_tensor(h_buf[:, :], a[:, :], found_f, h_buf[:, :], ALU.is_equal, ALU.mult)
                    eng.drain()
                    v.scalar_tensor_tensor(a[:, :], h_buf[:, :], -3e38, a[:, :], ALU.mult, ALU.add)
                    v.tensor_copy(keep, found_f)
                    eng.drain()
                with eng.Else():
                    eng.nop()
                eng.drain()

            def hidden(t, p, c):
                lo, hi = CH[c]
                v.scalar_tensor_tensor(h_buf[:, lo:hi], a_buf[p][:, lo:hi], keep, s_buf[p][:, lo:hi],
                                       ALU.is_ge, ALU.mult).then_inc(S("h_done"), 1)

            def h_low(t, g, b):
                eng.wait_ge(S("ht_hi"), 3 * t + g + 1)
                w, n = P * len(GRP[g]), len(GRP[g])
                v.tensor_tensor(ht_lo[b][:, 0:n, :], tp[g][:, 0:w].rearrange("p (k c) -> p k c", c=P),
                                ht_hi[b][:, 0:n, :], ALU.subtract).then_inc(S("ht_lo"), 1)

            def residual_add(t):
                eng.wait_ge(S("d_mm"), done("d_mm", 3 * t + 3))
                eng.wait_ge(S("xr_loaded"), 16 * t + 16)
                eng.wait_ge(S("x2_saved"), 16 * t + 16)
                v.tensor_tensor(x2[:, :], dn[:, :], x_res[:, :], ALU.add).then_inc(S("y_done"), 1)

            def mean_variance(t):
                eng.drain()
                v.bn_stats(stats, x2[:, :])
                eng.drain()
                v.bn_aggr(mv, stats)
                eng.drain()
                v.tensor_scalar(var_e, mv[:, 1:2], EPS, None, ALU.add).then_inc(S("var_done"), 1)

            def norm(t):
                eng.wait_ge(S("rstd"), t + 1)
                v.tensor_scalar(x2[:, :], x2[:, :], mv[:, 0:1], rstd, ALU.subtract, ALU.mult
                                ).then_inc(S("x2_done"), 1)
                eng.drain()
                hi = x16[:, bass.ds(t * 2 * HD, HD)]
                lo = x16[:, bass.ds(t * 2 * HD + HD, HD)]
                v.tensor_scalar(hi, x2[:, :], UP, None, ALU.mult)
                eng.drain()
                v.scalar_tensor_tensor(lo, x2[:, :], UP, hi, ALU.mult, ALU.subtract).then_inc(S("x16"), 1)

            for e in prologue():
                if e == ("mm", "g", 1, 0, 0):
                    eng.wait_ge(S("consts"), 1)
                if e[0] == "w":
                    if e[1] < 2 * N_WU:
                        weights_lo(e[1])
                elif e[0] == "x":
                    if e[1] < 2:
                        x_low(e[1], e[1])
                else:
                    _, kind, t, c, k = e
                    if kind == "u" and k == KB - 1:
                        up_times_s(0, 0, c)
            select(0, 0, 0)
            select(0, 0, 1)
            x_low(2, 0)
            select(0, 0, 2)
            up_times_s(1, 1, 0)
            select(0, 0, 3)
            up_times_s(1, 1, 1)
            select(0, 0, 4)
            up_times_s(1, 1, 2)
            settle(0, 0)
            for t in range(2):
                p, q = t % 2, 1 - t % 2
                for c in range(NC_):
                    hidden(t, p, c)
                if t:
                    norm(0)
                h_low(t, 0, p)
                h_low(t, 1, q)
                if t == 0:
                    x_low(3, 1)
                eng.wait_ge(S("ht_tr"), 3 * t + 3)
                select(t + 1, q, 0)
                if t:
                    h_low(t, 2, p)
                select(t + 1, q, 1)
                if t == 0:
                    h_low(t, 2, p)
                for part in range(2, 5):
                    select(t + 1, q, part)
                if t == 0:
                    residual_add(0)
                    mean_variance(0)
                    settle(1, 1)
            up_times_s(2, 0, 0)
            settle(2, 0)
            hidden(2, 0, 0)
            up_times_s(2, 0, 1)
            eng.drain()
            hidden(2, 0, 1)
            residual_add(1)
            h_low(2, 0, 0)
            up_times_s(2, 0, 2)
            mean_variance(1)
            eng.drain()
            hidden(2, 0, 2)

            def turn(t, p, more=True):
                q = 1 - p
                h_low(t, 1, q)
                if more:
                    x_low(t + 2, p)
                h_low(t, 2, p)
                norm(t - 1)
                if more:
                    select(t + 1, q)
                    up_times_s(t + 1, q, 0)
                else:
                    for part in range(4):
                        select(t + 1, q, part)
                    up_times_s(t + 1, q, 0)
                    up_times_s(t + 1, q, 1)
                    select(t + 1, q, 4)
                if more:
                    settle(t + 1, q)
                    hidden(t + 1, q, 0)
                    up_times_s(t + 1, q, 1)
                    eng.drain()
                    hidden(t + 1, q, 1)
                    residual_add(t)
                    h_low(t + 1, 0, q)
                up_times_s(t + 1, q, 2)
                if more:
                    mean_variance(t)
                    eng.drain()
                    hidden(t + 1, q, 2)

            turns(eng, turn)
            turn(NT - 2, 0, more=False)
            settle(NT - 1, 1)
            for c in range(NC_):
                hidden(NT - 1, 1, c)

            def h2_mul(q, p):
                eng.wait_ge(S("sg_done"), q + 1)
                eng.wait_ge(S("u2_mm"), q + 1)
                if not (isinstance(q, int) and q < 2):
                    eng.wait_ge(S("h2_hi"), q - 1)
                v.scalar_tensor_tensor(h2[p][:, :], u2[p][:, :], 1.0 / UP, sg[p][:, :], ALU.mult,
                                       ALU.mult).then_inc(S("h2_done"), 1)

            def h2_low(q, p):
                eng.wait_ge(S("h2_hi"), q + 1)
                n = slot(q, p)
                v.tensor_tensor(h2_lo[n][:, :], h2[p][:, :], h2_hi[n][:, :],
                                ALU.subtract).then_inc(S("h2_lo"), 1)

            residual_add(NT - 2)
            h_low(NT - 1, 0, (NT - 1) % 2)
            h_low(NT - 1, 1, NT % 2)
            mean_variance(NT - 2)
            h2_mul(0, 0)
            norm(NT - 2)
            h2_low(0, 0)
            h_low(NT - 1, 2, (NT - 1) % 2)
            h2_mul(1, 1)
            residual_add(NT - 1)
            mean_variance(NT - 1)
            h2_low(1, 1)
            norm(NT - 1)

            def step2(q, p, half):
                at_ = q if isinstance(q, int) else None
                if at_ in (0, 1):
                    return
                h2_mul(q, p)
                if at_ == MB:
                    residual(0, 0)
                    residual(0, 1)
                h2_low(q, p)
                if at_ == MB:
                    residual(0, 2)
                    residual(0, 3)
                if at_ in (MB, MB + 1):
                    for j in ((0, 1), (2, 3))[at_ - MB]:
                        statistics(j)
                    if at_ == MB + 1:
                        for j in range(TH):
                            normalise(0, j)

            def residual(half, j):
                n = TH * MB - TH + j + 1 if half == 0 else TH * LAST + KEEP * (j + 1)
                eng.wait_ge(S("dn_mm"), n)
                if j == 0:
                    eng.wait_ge(S("res"), 16 * TH * (half + 1))
                v.tensor_tensor(res[j][:, :], acc[j][:, :], res[j][:, :], ALU.add).then_inc(S("y2_done"), 1)

            def statistics(j):
                eng.drain()
                v.bn_stats(stats2, res[j][:, :])
                eng.drain()
                v.bn_aggr(mv2[j], stats2)
                eng.drain()
                v.tensor_scalar(var_e2[:, j:j + 1], mv2[j][:, 1:2], EPS, None, ALU.add
                                ).then_inc(S("var2_done"), 1)

            def normalise(half, j):
                eng.wait_ge(S("rstd2"), TH * half + j + 1)
                v.tensor_scalar(res[j][:, :], res[j][:, :], mv2[j][:, 0:1], rstd2[:, j:j + 1],
                                ALU.subtract, ALU.mult).then_inc(S("o_done"), 1)

            steps2(eng, step2)
            for j in range(TH):
                residual(1, j)
                if j == TH - 1:
                    normalise(1, j - 1)
                statistics(j)
                if 0 < j < TH - 1:
                    normalise(1, j - 1)
            normalise(1, TH - 1)

        @block.tensor
        def _(eng):
            eng.nop().then_inc(S("d_mm"), CR["d_mm"])

            def x_transpose(t, p):
                eng.wait_ge(S(f"x_loaded{p}"), 8 * t + 16 - 8 * p)
                if isinstance(t, int) and t < 4:
                    if t:
                        eng.wait_ge(S("xt_lo"), t)
                else:
                    eng.wait_ge(S("flag_read"), t - 1)
                for k in range(KB):
                    ins = eng.transpose(xb[:, P * k:P * k + P], x_in[p][:, P * k:P * k + P], ident[:, :])
                ins.then_inc(S("x_tr"), 1)

            def project(p, hi, lo, bk, c, k):
                a, b = CH[c]
                for i, (xt, w) in enumerate(((xt_hi[p], hi), (xt_hi[p], lo), (xt_lo[p], hi))):
                    ins = eng.matmul(bk[:, 0:b - a], xt[:, k, :], w[:, k, a:b],
                                     start=(k == 0 and i == 0), stop=(k == KB - 1 and i == 2))
                return ins

            def gate_block(t, p, c, k):
                at_ = t if isinstance(t, int) else None
                if at_ == 0:
                    eng.wait_ge(S("w_lo"), KB * c + k + 1)
                if k == 0:
                    if at_ == 1:
                        eng.wait_ge(S("g_act"), c + 1)
                    elif at_ == 3:
                        eng.wait_ge(S("g_act"), 6 + c + 1)
                    elif at_ != 0:
                        eng.wait_ge(S("u_mul"), 3 * t + c - 5)
                    if c == 0:
                        eng.wait_ge(S("xt_lo"), t + 1)
                ins = project(p, wg_hi, wg_lo, gu[c], c, k)
                if k == KB - 1:
                    ins.then_inc(S("g_mm"), 1)

            def gate(t, p, chunks=range(NC_)):
                for c in chunks:
                    for k in range(KB):
                        gate_block(t, p, c, k)

            def up_block(t, p, c, k):
                at_ = t if isinstance(t, int) else None
                if at_ == 0:
                    eng.wait_ge(S("w_lo"), N_WU + KB * c + k + 1)
                if k == 0:
                    if at_ == NT - 1:
                        eng.wait_ge(S("u_mul"), 3 * t - 3 + c + 1)
                    elif at_ != 1:
                        eng.wait_ge(S("g_act"), 3 * t + 3 + c + 1)
                ins = project(p, wu_hi, wu_lo, up_bank(t, c), c, k)
                if k == KB - 1:
                    ins.then_inc(S("u_mm"), 1)

            def up(t, p, c):
                for k in range(KB):
                    up_block(t, p, c, k)

            def count_good(t):
                if is_first(t):
                    eng.wait_ge(S("consts"), 1)
                eng.wait_ge(S("sel_done"), done("sel_done", t + 1))
                eng.matmul(good_bank(t)[0:1, 0:1], good, one_c, start=True, stop=True).then_inc(S("flag_mm"), 1)

            def h_transpose(t, g):
                eng.wait_ge(S("h_done"), 3 * t + g + 1)
                eng.wait_ge(S("ht_lo"), 3 * t + g + 1)
                for k, b in enumerate(GRP[g]):
                    ins = eng.transpose(tp[g][0:IW[b], P * k:P * k + P], h_buf[:, P * b:P * b + IW[b]],
                                        ident[:, :])
                ins.then_inc(S("ht_tr"), 1)

            def down(t, g, b_):
                eng.wait_ge(S("ht_lo"), done("ht_lo", 3 * t + g + 1))
                if is_first(t):
                    eng.wait_ge(S("wd_lo"), GRP[g][-1] + 1)
                if g == 0:
                    eng.wait_ge(S("y_done"), t + 1)
                for k, b in enumerate(GRP[g]):
                    w = IW[b]
                    hi, lo = ht_hi[b_][0:w, k, :], ht_lo[b_][0:w, k, :]
                    eng.matmul(dn[:, :], hi, wd_hi[0:w, b, :], start=(b == 0), stop=False)
                    eng.matmul(dn[:, :], hi, wd_lo[0:w, b, :], start=False, stop=False)
                    ins = eng.matmul(dn[:, :], lo, wd_hi[0:w, b, :], start=False, stop=(b == IB - 1))
                ins.then_inc(S("d_mm"), 1)

            eng.wait_ge(S("ident"), 1)
            for n in range(WARM):
                eng.transpose(tp[0][:, 0:P], ident[:, :], ident[:, :])
            for e in prologue():
                if e[0] == "x":
                    x_transpose(e[1], e[1] % 2)
                elif e[0] == "mm":
                    _, kind, t, c, k = e
                    (gate_block if kind == "g" else up_block)(t, t, c, k)
            for c in range(NC_):
                up(1, 1, c)
            x_transpose(3, 1)
            for t in range(2):
                p, q = t % 2, 1 - t % 2
                gate(t + 2, p, (0,))
                for k in range(KB):
                    gate_block(t + 2, p, 1, k)
                    if k == 1:
                        count_good(t)
                if t == 0:
                    eng.wait_ge(S("u_mul"), 6)
                for g in range(NC_):
                    h_transpose(t, g)
                gate(t + 2, p, (2,))
                down(t, 0, p)
                down(t, 1, q)
                down(t, 2, p)

            def up_and_first_transpose(t, p):
                up(t, p, 0)
                count_good(t)
                up(t, p, 1)
                h_transpose(t, 0)
                up(t, p, 2)

            up_and_first_transpose(2, 0)

            def turn(t, p, more=True):
                q = 1 - p
                if more:
                    x_transpose(t + 2, p)
                h_transpose(t, 1)
                down(t, 0, p)
                h_transpose(t, 2)
                down(t, 1, q)
                down(t, 2, p)
                if more:
                    gate(t + 2, p)
                    up_and_first_transpose(t + 1, q)

            turns(eng, turn)
            turn(NT - 2, 0, more=False)

            def gate_up2(q, m, p, half, which=(0, 1)):
                tok = slice(half * HALF, half * HALF + HALF)
                for w in which:
                    bk = (g2, u2)[w][p]
                    if not (isinstance(q, int) and q < 2):
                        eng.wait_ge(S(("sg_done", "h2_done")[w]), q - 1)
                    for k in range(KB):
                        for part in range(2):
                            ins = eng.matmul(bk[:, :], vgu[:, w * KB + k, bass.ds(m * P, P)],
                                             x2t[part][:, k, tok], start=(k + part == 0),
                                             stop=(k == KB - 1 and part == 1))
                    ins.then_inc(S(("g2_mm", "u2_mm")[w]), 1)

            def down2(q, m, p, j, first, last):
                if first and q:
                    eng.wait_ge(S("y2_done"), j + 1)
                c = slice(P * j, P * j + P)
                rhs = vd[:, bass.ds(m, 1), :].rearrange("p a c -> p (a c)")
                eng.matmul(acc[j][:, :], h2_hi[p][:, c], rhs, start=first, stop=False)
                eng.matmul(acc[j][:, :], h2_lo[p][:, c], rhs, start=False, stop=last
                           ).then_inc(S("dn_mm"), 1)

            def x2t_transpose(t):
                eng.wait_ge(S("x16"), t + 1)
                if t < 2:
                    eng.wait_ge(S("ht_lo"), done("ht_lo", 3 * (NT - 2) + 2 + t))
                elif t < NT - 2:
                    eng.wait_ge(S("x2t_ev"), t - 1)
                bk = x2t_bank(t)[:, :].bitcast(f16)
                for j in range(2 * KB):
                    ins = eng.transpose(bk[:, P * j:P * j + P],
                                        x16[:, t * 2 * HD + P * j:t * 2 * HD + P * j + P], ident16[:, :])
                ins.then_inc(S("x2t_tr"), 1)

            T = NT - 1
            for c in range(NC_):
                x2t_transpose(2 * c)
                x2t_transpose(2 * c + 1)
                up(T, 1, c)
            eng.wait_ge(S("vgu"), 32)
            eng.wait_ge(S("x2t_ev"), TH)
            eng.wait_ge(S("u_mul"), 3 * NT - 2)
            gate_up2(0, 0, 0, 0, (0,))
            eng.wait_ge(S("u_mul"), 3 * NT - 1)
            gate_up2(0, 0, 0, 0, (1,))
            count_good(T)
            eng.wait_ge(S("u_mul"), 3 * NT)
            gate_up2(1, 1, 1, 0)
            eng.wait_ge(S("flag_read"), NT)
            h_transpose(T, 0)
            eng.wait_ge(S("x2t_ev"), NT - 2)
            h_transpose(T, 1)
            gate_up2(2, 2, 0, 0, (0,))
            down(T, 0, 1)
            h_transpose(T, 2)
            down(T, 1, 0)
            down(T, 2, 1)

            def step2(q, p, half):
                m = q - half * MB
                at_ = q if isinstance(q, int) else None
                if at_ == MB - 2:
                    eng.wait_ge(S("sg_done"), q + 1)
                    x2t_transpose(NT - 2)
                if at_ == MB - 1:
                    eng.wait_ge(S("x2t_ev"), NT)
                    gate_up2(q + 1, 0, 1 - p, 1)
                elif at_ not in (0, 2 * MB - 1):
                    gate_up2(q + 1, m + 1, 1 - p, half, (1,) if at_ == 1 else (0, 1))
                if at_ == MB - 2:
                    eng.wait_ge(S("h2_done"), q + 1)
                    x2t_transpose(NT - 1)
                if at_ is not None and at_ >= LAST:
                    if at_ == 2 * MB - 1:
                        for j, b in ((j, b) for j in range(TH) for b in range(LAST, 2 * MB)):
                            eng.wait_ge(S("h2_lo"), b + 1)
                            down2(b, b - MB, b - LAST, j, False, b == at_)
                    return
                if half == 0:
                    eng.wait_ge(S("vd_ev"), q + 1)
                eng.wait_ge(S("h2_lo"), q + 1)
                for j in range(TH):
                    if at_ == 0 and j == TH - 1:
                        eng.wait_ge(S("y_done"), done("y_done", NT))
                    down2(q, m, p, j, at_ in (0, MB), at_ == MB - 1)

            steps2(eng, step2)


_INS = ['L0_attn_x', 'L0_attn_w_gate', 'L0_attn_w_up', 'L0_attn_w_down',
        'L0_ffn_W_gate', 'L0_ffn_W_up', 'L0_ffn_W_down']
_OUTS = [((4, 256, 512), 'float32')]


def kernel(**inputs):
    import numpy as _np
    import concourse.bacc as _bacc
    from concourse import mybir as _mybir
    from concourse.bass_utils import run_bass_kernel_spmd as _run

    nc = _bacc.Bacc("TRN2", target_bir_lowering=False, num_devices=1)
    arrays, args = {}, []
    for name in _INS:
        a = inputs[name] if name == "L0_attn_x" else _np.asarray(inputs[name]).T
        a = _np.ascontiguousarray(a)
        arrays[f"in_{name}_dram"] = a
        args.append(nc.dram_tensor(f"in_{name}_dram", a.shape, _mybir.dt.from_np(a.dtype), kind="ExternalInput").ap())
    for i, (shape, dtype) in enumerate(_OUTS):
        dt = _mybir.dt.from_np(_np.dtype(dtype))
        args.append(nc.dram_tensor(f"out_{i}_dram", shape, dt, kind="ExternalOutput").ap())
    build(nc, *args)
    r = _run(nc, [arrays], core_ids=[0])
    return r.results[0]["out_0_dram"]
```
